# Optimizing a Trainium2 kernel written in Bass

```python
import numpy as np
import jax
import jax.numpy as jnp

def _softmax(x, axis=-1):
    return jax.nn.softmax(x, axis=axis)

def _gelu(x):
    return jax.nn.gelu(x, approximate=True)

def _silu(x):
    return jax.nn.silu(x)

def _sigmoid(x):
    return jax.nn.sigmoid(x)

def _layernorm(x, axis=-1, eps=1e-05):
    m = jnp.mean(x, axis=axis, keepdims=True)
    v = jnp.var(x, axis=axis, keepdims=True)
    return (x - m) / jnp.sqrt(v + eps)

def _scatter_add(tgt, idx, src, axis=0):
    return tgt.at[idx].add(src)

def _segment_sum(src, seg, n):
    return jax.ops.segment_sum(src, seg, n)
kernel_name = 'mk_lm_tower_d1_tok_ids256_r4_776507'

def setup_inputs(seed: int=0):
    np.random.seed(seed)
    _w = jnp.asarray

    def _rec_inputs():
        import jax
        import jax.numpy as jnp
        _rk = jax.random.key(seed)
        x = jax.random.randint(jax.random.fold_in(_rk, 1), (8, 2048), 0, 127998, jnp.int32)
        return x
    x = _rec_inputs()

    def _L0_tok_setup():
        import jax, jax.numpy as jnp
        import numpy as np
        VOCAB = 32000
        HIDDEN = 512
        BATCH, SEQ = (4, 1024)
        key = jax.random.key(seed)
        k_ids, k_tab = jax.random.split(key)
        input_ids = jax.random.randint(k_ids, (BATCH, SEQ), 0, VOCAB, dtype=jnp.int32)
        ple_table = jax.random.normal(k_tab, (VOCAB, HIDDEN), dtype=jnp.float32)
        return {'input_ids': input_ids, 'ple_table': ple_table, 'layer_idx': 3, 'ple_dim': 64}
    _L0_tok_all = _L0_tok_setup()
    _L0_tok_in = {k: v for k, v in _L0_tok_all.items() if k in ('ple_table',)}
    del _L0_tok_all

    def _L0_attn_setup():
        import jax, jax.numpy as jnp
        import numpy as np
        HEAD_SIZE = 64
        HEAD_SIZE_R = HEAD_SIZE // 4
        HEAD_SIZE_C = HEAD_SIZE - HEAD_SIZE_R
        N_EMBD = 64

        def rope(x, start_pos=0):
            B, T, d = x.shape
            half = d // 2
            theta = 1.0 / 10000.0 ** (jnp.arange(half, dtype=x.dtype) / half)
            idx = jnp.arange(start_pos, start_pos + T, dtype=x.dtype)[:, None] * theta[None, :]
            sin, cos = (jnp.sin(idx), jnp.cos(idx))
            xs = x.reshape(B, T, half, 2)
            x1, x2 = (xs[..., 0], xs[..., 1])
            rot = jnp.stack([x1 * cos - x2 * sin, x1 * sin + x2 * cos], axis=-1)
            return rot.reshape(B, T, d)

        def _reference_tuple_inner(x, Wq_comp, Wkv_comp, Wqc, Wqr, Wkc, Wkr, Wv):
            c_q = x @ Wq_comp
            c_kv = x @ Wkv_comp
            q_c = c_q @ Wqc
            q_r = rope(c_q @ Wqr, start_pos=0)
            q = jnp.concatenate([q_c, q_r], axis=-1)
            k_c = c_kv @ Wkc
            k_r = rope(c_kv @ Wkr, start_pos=0)
            k = jnp.concatenate([k_c, k_r], axis=-1)
            v = c_kv @ Wv
            scale = 1.0 / jnp.sqrt(jnp.asarray(HEAD_SIZE, dtype=x.dtype))
            wei = jnp.einsum('bqd,bkd->bqk', q, k) * scale
            T_q = q.shape[1]
            mask = jnp.tril(jnp.ones((T_q, T_q), dtype=bool))
            wei = jnp.where(mask, wei, jnp.asarray(-jnp.inf, dtype=wei.dtype))
            wei = jax.nn.softmax(wei, axis=-1)
            out = jnp.einsum('bqk,bkd->bqd', wei, v)
            return (out, (k, v))
        key = jax.random.key(seed)
        ks = jax.random.split(key, 8)
        B, T = (32, 512)
        s = 0.05
        return {'x': jax.random.normal(ks[0], (B, T, N_EMBD), dtype=jnp.float32), 'Wq_comp': jax.random.normal(ks[1], (N_EMBD, N_EMBD), dtype=jnp.float32) * s, 'Wkv_comp': jax.random.normal(ks[2], (N_EMBD, N_EMBD), dtype=jnp.float32) * s, 'Wqc': jax.random.normal(ks[3], (N_EMBD, HEAD_SIZE_C), dtype=jnp.float32) * s, 'Wqr': jax.random.normal(ks[4], (N_EMBD, HEAD_SIZE_R), dtype=jnp.float32) * s, 'Wkc': jax.random.normal(ks[5], (N_EMBD, HEAD_SIZE_C), dtype=jnp.float32) * s, 'Wkr': jax.random.normal(ks[6], (N_EMBD, HEAD_SIZE_R), dtype=jnp.float32) * s, 'Wv': jax.random.normal(ks[7], (N_EMBD, HEAD_SIZE), dtype=jnp.float32) * s}
    _L0_attn_all = _L0_attn_setup()
    _L0_attn_in = {k: v for k, v in _L0_attn_all.items() if k in ('Wq_comp', 'Wkv_comp', 'Wqc', 'Wqr', 'Wkc', 'Wkr', 'Wv')}
    del _L0_attn_all

    def _L0_ffn_setup():
        import jax, jax.numpy as jnp
        import numpy as np
        B, T, IN_DIM = (64, 64, 64)
        HID, OUT_DIM = (128, 64)
        N_LAYERS, N_EXPERTS, N_SHARED = (2, 16, 1)
        key = jax.random.key(seed)
        ks = jax.random.split(key, 10)
        s = 0.02
        x = jax.random.normal(ks[0], (B, T, IN_DIM), dtype=jnp.float32)
        route_id = jax.random.randint(ks[1], (B,), 0, N_EXPERTS)
        Wi = jax.random.normal(ks[2], (HID, IN_DIM), dtype=jnp.float32) * s
        bi = jnp.zeros((HID,), dtype=jnp.float32)
        Wr = jax.random.normal(ks[3], (N_LAYERS, N_EXPERTS, HID, HID), dtype=jnp.float32) * s
        br = jax.random.normal(ks[4], (N_LAYERS, N_EXPERTS, HID), dtype=jnp.float32) * s
        Ws = jax.random.normal(ks[5], (N_LAYERS, N_SHARED, HID, HID), dtype=jnp.float32) * s
        bs = jax.random.normal(ks[6], (N_LAYERS, N_SHARED, HID), dtype=jnp.float32) * s
        Wo = jax.random.normal(ks[7], (OUT_DIM, HID), dtype=jnp.float32) * s
        bo = jnp.zeros((OUT_DIM,), dtype=jnp.float32)
        return {'x': x, 'route_id': route_id, 'Wi': Wi, 'bi': bi, 'Wr': Wr, 'br': br, 'Ws': Ws, 'bs': bs, 'Wo': Wo, 'bo': bo}
    _L0_ffn_all = _L0_ffn_setup()
    _L0_ffn_in = {k: v for k, v in _L0_ffn_all.items() if k in ('route_id', 'Wi', 'bi', 'Wr', 'br', 'Ws', 'bs', 'Wo', 'bo')}
    del _L0_ffn_all
    return {'x': x, 'L0_tok_ple_table': _L0_tok_in['ple_table'], 'L0_attn_Wq_comp': _L0_attn_in['Wq_comp'], 'L0_attn_Wkv_comp': _L0_attn_in['Wkv_comp'], 'L0_attn_Wqc': _L0_attn_in['Wqc'], 'L0_attn_Wqr': _L0_attn_in['Wqr'], 'L0_attn_Wkc': _L0_attn_in['Wkc'], 'L0_attn_Wkr': _L0_attn_in['Wkr'], 'L0_attn_Wv': _L0_attn_in['Wv'], 'L0_ffn_route_id': _L0_ffn_in['route_id'], 'L0_ffn_Wi': _L0_ffn_in['Wi'], 'L0_ffn_bi': _L0_ffn_in['bi'], 'L0_ffn_Wr': _L0_ffn_in['Wr'], 'L0_ffn_br': _L0_ffn_in['br'], 'L0_ffn_Ws': _L0_ffn_in['Ws'], 'L0_ffn_bs': _L0_ffn_in['bs'], 'L0_ffn_Wo': _L0_ffn_in['Wo'], 'L0_ffn_bo': _L0_ffn_in['bo']}

def reference(x, L0_tok_ple_table, L0_attn_Wq_comp, L0_attn_Wkv_comp, L0_attn_Wqc, L0_attn_Wqr, L0_attn_Wkc, L0_attn_Wkr, L0_attn_Wv, L0_ffn_route_id, L0_ffn_Wi, L0_ffn_bi, L0_ffn_Wr, L0_ffn_br, L0_ffn_Ws, L0_ffn_bs, L0_ffn_Wo, L0_ffn_bo):
    import jax
    import jax.numpy as jnp

    def _L0_tok_ref(input_ids, ple_table, layer_idx, ple_dim):
        import jax, jax.numpy as jnp
        import numpy as np
        VOCAB = 32000
        HIDDEN = 512
        BATCH, SEQ = (4, 1024)
        start = layer_idx * ple_dim
        layer_slice = jax.lax.dynamic_slice_in_dim(ple_table, start, ple_dim, axis=1)
        return layer_slice[input_ids].astype(jnp.float32)

    def _L0_attn_ref(x, Wq_comp, Wkv_comp, Wqc, Wqr, Wkc, Wkr, Wv):
        import jax, jax.numpy as jnp
        import numpy as np
        HEAD_SIZE = 64
        HEAD_SIZE_R = HEAD_SIZE // 4
        HEAD_SIZE_C = HEAD_SIZE - HEAD_SIZE_R
        N_EMBD = 64

        def rope(x, start_pos=0):
            B, T, d = x.shape
            half = d // 2
            theta = 1.0 / 10000.0 ** (jnp.arange(half, dtype=x.dtype) / half)
            idx = jnp.arange(start_pos, start_pos + T, dtype=x.dtype)[:, None] * theta[None, :]
            sin, cos = (jnp.sin(idx), jnp.cos(idx))
            xs = x.reshape(B, T, half, 2)
            x1, x2 = (xs[..., 0], xs[..., 1])
            rot = jnp.stack([x1 * cos - x2 * sin, x1 * sin + x2 * cos], axis=-1)
            return rot.reshape(B, T, d)

        def _reference_tuple_inner(x, Wq_comp, Wkv_comp, Wqc, Wqr, Wkc, Wkr, Wv):
            c_q = x @ Wq_comp
            c_kv = x @ Wkv_comp
            q_c = c_q @ Wqc
            q_r = rope(c_q @ Wqr, start_pos=0)
            q = jnp.concatenate([q_c, q_r], axis=-1)
            k_c = c_kv @ Wkc
            k_r = rope(c_kv @ Wkr, start_pos=0)
            k = jnp.concatenate([k_c, k_r], axis=-1)
            v = c_kv @ Wv
            scale = 1.0 / jnp.sqrt(jnp.asarray(HEAD_SIZE, dtype=x.dtype))
            wei = jnp.einsum('bqd,bkd->bqk', q, k) * scale
            T_q = q.shape[1]
            mask = jnp.tril(jnp.ones((T_q, T_q), dtype=bool))
            wei = jnp.where(mask, wei, jnp.asarray(-jnp.inf, dtype=wei.dtype))
            wei = jax.nn.softmax(wei, axis=-1)
            out = jnp.einsum('bqk,bkd->bqd', wei, v)
            return (out, (k, v))
        return _reference_tuple_inner(x, Wq_comp, Wkv_comp, Wqc, Wqr, Wkc, Wkr, Wv)[0]

    def _L0_ffn_ref(x, route_id, Wi, bi, Wr, br, Ws, bs, Wo, bo):
        import jax, jax.numpy as jnp
        import numpy as np
        B, T, IN_DIM = (64, 64, 64)
        HID, OUT_DIM = (128, 64)
        N_LAYERS, N_EXPERTS, N_SHARED = (2, 16, 1)
        flat = x.reshape(-1, x.shape[-1])
        n_tok = flat.shape[0]
        route = jnp.repeat(route_id, n_tok // route_id.shape[0])
        h = jax.nn.relu(flat @ Wi.T + bi)
        n_layers, n_experts = (Wr.shape[0], Wr.shape[1])
        for l in range(n_layers):
            shared = (jnp.einsum('nd,shd->snh', h, Ws[l]) + bs[l][:, None, :]).mean(axis=0)
            routed = jnp.zeros_like(h)
            for e in range(n_experts):
                ye = h @ Wr[l, e].T + br[l, e]
                routed = routed + jnp.where((route == e)[:, None], ye, 0.0)
            h = jax.nn.relu(shared + routed + h)
        out = h @ Wo.T + bo
        return out.reshape(*x.shape[:-1], out.shape[-1])
    h = _L0_tok_ref(x, L0_tok_ple_table, 3, 64)
    h = h + _L0_attn_ref(_layernorm(h, axis=-1), L0_attn_Wq_comp, L0_attn_Wkv_comp, L0_attn_Wqc, L0_attn_Wqr, L0_attn_Wkc, L0_attn_Wkr, L0_attn_Wv)
    h = h + _L0_ffn_ref(_layernorm(h, axis=-1), L0_ffn_route_id, L0_ffn_Wi, L0_ffn_bi, L0_ffn_Wr, L0_ffn_br, L0_ffn_Ws, L0_ffn_bs, L0_ffn_Wo, L0_ffn_bo)
    return h

_drawn_inputs = setup_inputs


def setup_inputs(seed=0):
    import zlib

    import numpy as np

    out = dict(_drawn_inputs(seed))
    spreads = {'L0_ffn_bi': (0.0, 0.504), 'L0_ffn_bo': (0.0, 0.1)}
    factors = {'L0_attn_Wq_comp': 8.0,
     'L0_attn_Wqc': 8.0,
     'L0_attn_Wqr': 8.0,
     'L0_attn_Wkc': 8.0,
     'L0_attn_Wkr': 8.0,
     'L0_ffn_Wi': 2.679,
     'L0_ffn_Wr': 6.872,
     'L0_ffn_br': 8.0,
     'L0_ffn_Ws': 6.622,
     'L0_ffn_bs': 8.0}
    for name, (base, spread) in spreads.items():
        noise = np.random.default_rng([zlib.crc32(name.encode()), seed]).standard_normal(out[name].shape)
        drawn = base * np.exp(spread * noise) if base else spread * noise
        out[name] = jnp.asarray(drawn.astype(out[name].dtype))
    for name, factor in factors.items():
        out[name] = (out[name] * factor).astype(out[name].dtype)
    return out
```

```python
from contextlib import ExitStack

import concourse.bass as bass
import numpy as np
from concourse import mybir
from concourse.alu_op_type import AluOpType as ALU

ACT = mybir.ActivationFunctionType
AX = mybir.AxisListType
F32 = mybir.dt.float32
F32R = mybir.dt.float32r
BF16 = mybir.dt.bfloat16
I32 = mybir.dt.int32

P = 128
D = 64
BATCH, SEQ = 8, 2048
VOCAB, HIDDEN = 32000, 512
SLICE = 3
ROPE = 16
HID, N_LAYERS, N_EXPERTS = 128, 2, 16
ROUTED = BATCH * SEQ // 64
EPS = 1e-5

TILES = SEQ // P
QB = 512
BLOCKS = SEQ // QB
TPB = QB // P
EW = N_LAYERS * HID + N_LAYERS
WOW = 96
NEG = -1e30


def attention_chunks():
    chunks = []
    for i in range(BLOCKS):
        for kt in range(0, TPB * i, 2):
            chunks.append((i, [(kt, 0, QB, 0, ""), (kt + 1, 0, QB, QB, "")]))
        k = TPB * i
        chunks.append((i, [(k, 0, 512, 0, "edge"), (k + 1, 128, 384, 512, "edge")]))
        chunks.append((i, [(k + 2, 256, 256, 0, "edge"), (k + 3, 256, 256, 256, "full+edge")]))
    return chunks


CHUNKS = attention_chunks()
NS = len(CHUNKS)
LAST = [max(n for n, ch in enumerate(CHUNKS) if ch[0] == i) for i in range(BLOCKS)]
PBUF = 2


def max_pieces():
    return [(t, g) for t in range(TILES) for g in range(t // TPB + 1)]


PIECES = max_pieces()
NM = len(PIECES)

T_EVENTS = sorted(
    [(3 * c + 2, 0, "xT", c) for c in range(BLOCKS)]
    + [(3 * c + 3, 0, "proj", c) for c in range(BLOCKS)]
    + [(3 * c + 5, 1, "kT", c) for c in range(BLOCKS)]
    + [(3 * c + 6, 1, "qT", c) for c in range(BLOCKS)]
    + [(s, 1, "mT", c) for c, s in enumerate((10, 14, NS, NS + 8))]
)
NT = len(T_EVENTS)
T_ORDER = [(k, c) for _, _, _, k, c in sorted((s % NS, pt, s >= NS, k, c) for s, pt, k, c in T_EVENTS)]
T_TAIL = [(k, c) for s, _, k, c in T_EVENTS if s >= NS]
MAX_AT = {8: 2, 9: 2, 11: 3, 12: 3, 13: 2, 15: 3, 16: 3, 17: 2, 18: 2, 19: 2}
MAX_AT.update({NS + n: 2 for n in range(8)})
F_EVENTS = sorted(
    [(s, 0, "attn", i) for i, s in enumerate((3, 7, 13))]
    + [(1, 0, "attn", 3)]
    + [(min(7 + 3 * c + j, NS - 1), int(j < 3 or (c == 3 and j == 4)), k, c)
       for c in range(BLOCKS) for j, k in enumerate(("x2T", "in", "mlp0", "mlp1", "out"))],
    key=lambda e: (e[0], e[1], -["attn", "x2T", "in", "mlp0", "mlp1", "out"].index(e[2]) if e[2] != "attn" else -9))
NF = len(F_EVENTS)
NF0 = 3
F_ORD = {(k, c): n for n, (_, _, k, c) in enumerate(F_EVENTS)}
F_ORD0 = {("attn", i): i for i in range(3)}


def tower_kernel(nc, ids, table, consts, rope, small, wi, wo, wr, ws, brt, bst, bi, bo, route, out):
    table_rows = table.rearrange("v (s d) -> (v s) d", d=D)
    out_v = out.rearrange("b (t p) d -> b p t d", p=P)

    with ExitStack() as ctx:
        def sb(name, shape, dt=F32):
            return ctx.enter_context(nc.sbuf_tensor(name, shape, dt))

        def bank(name, n=1):
            return ctx.enter_context(nc.psum_tensor(name, [P, 512 * n], F32))

        def sem(name):
            return ctx.enter_context(nc.semaphore(name))

        con = sb("con", [P, 4 * P])
        ident = con[:, 0:P]
        conb = sb("conb", [P, 4 * P], BF16)
        identb, full_edge, edge, edge_q = conb[:, 0:P], conb[:, P:3 * P], conb[:, 2 * P:3 * P], conb[:, 3 * P:4 * P]
        rope_sb = sb("rope_sb", [P, 2, TILES, 2, ROPE])
        sm = sb("sm", [D, 448])
        smc = sb("smc", [D, P])
        wqk = sb("wqk", [P, P])
        wv = sb("wv", [P, P])
        wi_sb = sb("wi_sb", [P, HID])
        wi_h = sb("wi_h", [P, HID], F32R)
        wi_l = sb("wi_l", [P, HID], F32R)
        wo_sb = sb("wo_sb", [P, WOW])
        experts = sb("experts", [P, N_EXPERTS + 1, EW])
        bi_sb = sb("bi_sb", [P, 1])
        bo_sb = sb("bo_sb", [P, D])
        route_i = sb("route_i", [1, 64], I32)
        route_f = sb("route_f", [1, 3, 64])
        route_e = sb("route_e", [1, 64], I32)
        ids_i = sb("ids_i", [P, P], I32)
        ids_f = sb("ids_f", [P, 2, P])
        rows_all = sb("rows_all", [P, P + TILES], I32)
        rows_now = sb("rows_now", [P, TILES], I32)
        gate = sb("gate", [P, 1])
        lnc = sb("lnc", [P, 3])
        G = [sb(f"G{n}", [P, TILES, D]) for n in range(2)]
        Hres = [sb(f"Hres{n}", [P, TILES, D]) for n in range(2)]
        xn = [sb(f"xn{n}", [P, TILES, D]) for n in range(2)]
        sq = sb("sq", [P, TILES, D])
        stat = [sb(f"stat{n}", [P, 6, TILES]) for n in range(2)]
        Xs = [sb(f"Xs{n}", [P, TILES, P], F32R) for n in range(2)]
        XT = sb("XT", [P, QB])
        QK = sb("QK", [P, TPB, P])
        rt = sb("rt", [P, 2, TPB, 2, ROPE])
        QKs = sb("QKs", [P, TPB, 4 * D], F32R)
        QT = sb("QT", [P, QB], F32R)
        K1 = [sb(f"K1{n}", [P, SEQ], F32R) for n in range(2)]
        K2 = [sb(f"K2{n}", [P, SEQ], F32R) for n in range(2)]
        Q1 = [sb(f"Q1{n}", [P, SEQ], F32R) for n in range(2)]
        Q2 = [sb(f"Q2{n}", [P, SEQ], F32R) for n in range(2)]
        pm = [sb(f"pm{n}", [P, TPB, BLOCKS]) for n in range(2)]
        nm = [sb(f"nm{n}", [P, TPB]) for n in range(2)]
        mrow = sb("mrow", [TPB, P], F32R)
        prob = [sb(f"prob{n}", [P, 1024]) for n in range(PBUF)]
        YS = sb("YS", [P, QB])
        rec = sb("rec", [P, TPB])
        att = sb("att", [P, TPB, D])
        H1 = [sb(f"H1{n}", [P, TILES, D]) for n in range(2)]
        H1b = sb("H1b", [P, TILES, D])
        X2s = sb("X2s", [P, TILES, P], F32R)
        X2T = sb("X2T", [P, QB], F32R)
        hid = [sb(f"hid{n}", [P, QB]) for n in range(3)]
        wexp = [sb(f"wexp{n}", [P, 2, EW]) for n in range(2)]
        O = [sb(f"O{n}", [P, TPB, D]) for n in range(2)]

        S = [bank(f"S{n}", 2) for n in range(2)]
        Y = bank("Y")
        M = bank("M")
        T = bank("T")
        F = bank("F")

        load = sem("load")
        load2 = sem("load2")
        ready = sem("ready")
        folded = sem("folded")
        rows_ready = sem("rows_ready")
        gathered = sem("gathered")
        hres_in = sem("hres_in")
        ln_sum = [sem(f"ln_sum{n}") for n in range(2)]
        ln_xc = [sem(f"ln_xc{n}") for n in range(2)]
        ln_var = [sem(f"ln_var{n}") for n in range(2)]
        ln_sq = [sem(f"ln_sq{n}") for n in range(2)]
        ln_x = [sem(f"ln_x{n}") for n in range(2)]
        ln_h = [sem(f"ln_h{n}") for n in range(2)]
        ln_l = [sem(f"ln_l{n}") for n in range(2)]
        ones_in = sem("ones_in")
        roped = sem("roped")
        split = sem("split")
        dup = [sem(f"dup{n}") for n in range(2)]
        mrow_in = sem("mrow_in")
        nm_ready = sem("nm_ready")
        s_full, p_ready, p_used = sem("s_full"), sem("p_ready"), sem("p_used")
        y_free = sem("y_free")
        m_full, m_free = sem("m_full"), sem("m_free")
        t_full, t_free = sem("t_full"), sem("t_free")
        f_full, f_free = sem("f_full"), sem("f_free")
        h1_done = sem("h1_done")
        h1b_ready = sem("h1b_ready")
        w_in = [sem(f"w_in{n}") for n in range(2)]
        out_dma = [sem(f"out_dma{n}") for n in range(2)]

        def due(n):
            return not isinstance(n, int) or n > 0

        def t_at(k, c, b):
            tail = (k, c) in T_TAIL
            if isinstance(b, int) and b == 0 and not tail:
                return [o for o in T_ORDER if o not in T_TAIL].index((k, c))
            n = T_ORDER.index((k, c))
            if isinstance(b, int) and b == BATCH - 1 and tail:
                n = T_TAIL.index((k, c))
            return NT * (b + tail) - len(T_TAIL) + n

        def f_at(k, c, it):
            if isinstance(it, int) and it == 0:
                return F_ORD0[k, c]
            n = F_ORD[k, c]
            if isinstance(it, int) and it == BATCH and k != "attn":
                n -= sum(1 for i in range(3) if F_ORD["attn", i] < n)
            return NF * it + (NF0 - NF) + n

        def piece_at(step, tail):
            s = step + NS * tail
            if s not in MAX_AT:
                return []
            first = sum(n for x, n in MAX_AT.items() if x < s)
            return list(range(first, first + MAX_AT[s]))

        def iteration(step_of, b, par):
            for s in range(NS):
                step_of(b, par, s)

        def run(eng, prologue, step_of):
            prologue()
            for b in (-2, -1, 0):
                iteration(step_of, b, b % 2)
            with eng.Fori(0, 3) as j:
                iteration(step_of, j * 2 + 1, 1)
                iteration(step_of, j * 2 + 2, 0)
            for b in (7, 8):
                iteration(step_of, b, b % 2)

        def on(b):
            if not isinstance(b, int):
                return True, True, True, True
            return 0 <= b < BATCH, 0 < b <= BATCH, -1 <= b < BATCH - 1, b < BATCH - 2

        block = ctx.enter_context(nc.Block())

        @block.sync
        def _(sp):
            def prologue():
                sp.dma_start(ids_i[:, :], ids).then_inc(load, 16)
                sp.dma_start(con[:, :], consts).then_inc(load, 16)
                sp.dma_start(sm[:, :], small).then_inc(load, 16)
                sp.dma_start(rope_sb[:, :, :, :, :], rope).then_inc(load2, 16)
                sp.dma_start(route_i[:, :], route).then_inc(load2, 16)
                sp.dma_start(wi_sb[:, :], wi).then_inc(load2, 16)
                sp.dma_start(bi_sb[:, :], bi).then_inc(load2, 16)
                sp.dma_start(bo_sb[:, :], bo).then_inc(load2, 16)
                sp.wait_ge(ready, 1)
                sp.dma_start(wo_sb[:, 0:D], wo).then_inc(load2, 16)
                sp.dma_start(experts[:, N_EXPERTS, 0:2 * HID], ws).then_inc(load2, 16)
                sp.dma_start(experts[:, N_EXPERTS, 2 * HID:EW], bst).then_inc(load2, 16)
                sp.dma_start(experts[:, 0:N_EXPERTS, 0:2 * HID], wr).then_inc(load2, 16)
                sp.dma_start(experts[:, 0:N_EXPERTS, 2 * HID:EW], brt).then_inc(load2, 16)

            def step(b, par, s):
                attends, before, prepares, _ = on(b)
                if s == 2 and prepares:
                    if isinstance(b, int):
                        sp.wait_ge(gathered, 256 * (b + 2))
                    if due(4 * b):
                        sp.wait_ge(h1_done, 4 * b)
                    sp.dma_start(Hres[1 - par][:, :, :], G[1 - par][:, :, :]).then_inc(hres_in, 16)
                for (ev, _, k, c) in T_EVENTS:
                    if ev == s and prepares:
                        nb = b + 1
                        cols = slice(QB * c, QB * c + QB)
                        if k == "kT":
                            sp.wait_ge(t_free, t_at("kT", c, nb) + 1)
                            sp.dma_start(K2[1 - par][0:D, cols].bitcast(F32),
                                         K1[1 - par][0:D, cols].bitcast(F32)).then_inc(dup[c % 2], 16)
                        if k == "qT":
                            sp.wait_ge(t_free, t_at("qT", c, nb) + 1)
                            for dst, src in ((Q1[1 - par][0:D, cols], QT[D:P, :]), (Q1[1 - par][D:P, cols], QT[D:P, :]),
                                             (Q2[1 - par][0:D, cols], QT[0:D, :])):
                                sp.dma_start(dst.bitcast(F32), src.bitcast(F32)).then_inc(dup[c % 2], 16)
                    tail = ev - NS == s and attends
                    if (ev == s and prepares or tail) and k == "mT":
                        nb, q = (b, par) if tail else (b + 1, 1 - par)
                        sp.wait_ge(t_free, t_at("mT", c, nb) + 1)
                        sp.dma_start(Q2[q][D:D + 1, QB * c:QB * c + QB].bitcast(F32),
                                     mrow[:, :].bitcast(F32)).then_inc(mrow_in, 16)
                for (ev, _, k, c) in F_EVENTS:
                    if k == "x2T" and s == ev - 4 and before:
                        if c >= 2:
                            sp.wait_ge(f_free, f_at("mlp1", c - 2, b) + 1)
                        for r in range(2):
                            e = sp.value_load(route_e[0:1, bass.ds(8 * (b - 1) + 2 * c + r, 1)],
                                              min_val=0, max_val=N_EXPERTS)
                            sp.dma_start(wexp[c % 2][:, r, :], experts[:, bass.ds(e, 1), :].rearrange(
                                "p a n -> p (a n)")).then_inc(w_in[c % 2], 16)
                    if k == "out" and s == ev and before:
                        sp.wait_ge(f_free, f_at("out", c, b) + 1)
                        sp.dma_start(out_v[bass.ds(b - 1, 1), :, TPB * c:TPB * c + TPB, :].rearrange(
                            "a p t d -> (a p) t d"), O[c % 2][:, :, :]).then_inc(out_dma[c % 2], 16)

            def first():
                prologue()
                sp.wait_ge(ready, 4)
            run(sp, first, step)
            for n in range(2):
                sp.wait_ge(out_dma[n], 16 * (2 * BATCH + 1))

        @block.gpsimd
        def _(pool):
            def prologue():
                nc.gpsimd.memset(gate[:, :], 0.0)
                for n, x in enumerate((1.0 / D, EPS, -0.5)):
                    nc.gpsimd.memset(lnc[:, n:n + 1], x)
                nc.gpsimd.drain()

            def centre(n, src):
                p, st = nc.gpsimd, stat[n]
                p.tensor_tensor(st[:, 1, :], st[:, 0, :], lnc[:, 0:1].broadcast_to([P, TILES]), ALU.mult)
                p.drain()
                p.tensor_tensor(xn[n][:, :, :], src, st[:, 1, :].unsqueeze(2).broadcast_to([P, TILES, D]),
                                ALU.subtract).then_inc(ln_xc[n], 1)

            def normalise(n):
                p, st = nc.gpsimd, stat[n]
                for row, op in ((2, ALU.mult), (3, ALU.add), (4, ALU.pow)):
                    p.tensor_tensor(st[:, row + 1, :], st[:, row, :],
                                    lnc[:, row - 2:row - 1].broadcast_to([P, TILES]), op)
                    p.drain()
                p.tensor_tensor(xn[n][:, :, :], xn[n][:, :, :],
                                st[:, 5, :].unsqueeze(2).broadcast_to([P, TILES, D]), ALU.mult).then_inc(ln_x[n], 1)

            def low_part(n, xs):
                nc.gpsimd.tensor_tensor(xs[:, :, D:P], xn[n][:, :, :], xs[:, :, 0:D].bitcast(F32),
                                        ALU.subtract).then_inc(ln_l[n], 1)

            def step(b, par, s):
                attends, before, prepares, looks = on(b)
                if s == 1 and prepares:
                    pool.wait_ge(ln_h[0], b + 2)
                    low_part(0, Xs[1 - par])
                if s == 2 and before:
                    pool.wait_ge(ln_sum[1], b)
                    centre(1, H1[1 - par][:, :, :])
                if s == 5 and before:
                    pool.wait_ge(ln_var[1], b)
                    normalise(1)
                if s == 7 and before:
                    pool.wait_ge(ln_h[1], b)
                    low_part(1, X2s)
                if s == 12 and looks:
                    pool.wait_ge(ln_sum[0], b + 3)
                    centre(0, G[par][:, :, :])
                if s == 15 and looks:
                    pool.wait_ge(ln_var[0], b + 3)
                    normalise(0)
                if s == 3 and before:
                    pool.wait_ge(h1_done, 4 * b)
                    if not isinstance(b, int) or b > 1:
                        pool.wait_ge(f_free, f_at("out", 3, b - 1) + 1)
                    nc.gpsimd.tensor_tensor(H1b[:, :, :], H1[1 - par][:, :, :],
                                            bo_sb[:, :].unsqueeze(1).broadcast_to([P, TILES, D]),
                                            ALU.add).then_inc(h1b_ready, 1)
                if 8 <= s < 12 and looks:
                    if s == 8:
                        pool.wait_ge(rows_ready, b + 3)
                        if due(16 * (b + 1)):
                            pool.wait_ge(hres_in, 16 * (b + 1))
                        nc.gpsimd.tensor_tensor(gate[:, :], gate[:, :], gate[:, :], ALU.mult)
                    for t in range(4 * (s - 8), 4 * (s - 8) + 4):
                        nc.gpsimd.indirect_dma_start(
                            out=G[par][:, t, :], out_offset=None, in_=table_rows,
                            in_offset=bass.IndirectOffsetOnAxis(ap=rows_now[:, t:t + 1], axis=0),
                        ).then_inc(gathered, 16)
                for (ev, _, k, c) in T_EVENTS:
                    if k == "proj" and ev == s and prepares:
                        nb = b + 1
                        pool.wait_ge(t_free, t_at("proj", c, nb) + 1)
                        r = QK[:, :, :].rearrange("p t (a d) -> p t a d", a=2)[:, :, :, D - ROPE:D]
                        cos, sin = (rope_sb[:, n, TPB * c:TPB * c + TPB] for n in range(2))
                        for half in range(2):
                            nc.gpsimd.tensor_tensor(rt[:, 1, :, :, half::2], r[:, :, :, 1 - half::2],
                                                    sin[:, :, :, half::2], ALU.mult)
                        nc.gpsimd.tensor_tensor(rt[:, 0], r, cos, ALU.mult)
                        nc.gpsimd.drain()
                        nc.gpsimd.tensor_tensor(r, rt[:, 0], rt[:, 1], ALU.add).then_inc(roped, 1)
            run(pool, prologue, step)

        @block.scalar
        def _(act):
            def prologue():
                pass

            def relu(dst, src, bias):
                return nc.scalar.activation(dst, src, ACT.Relu, bias=bias)

            def step(b, par, s):
                attends, before, prepares, looks = on(b)
                if attends:
                    n = NS * b + s
                    i, parts = CHUNKS[s]
                    width = parts[-1][3] + parts[-1][2]
                    act.wait_ge(s_full, n + 1)
                    if due(n - PBUF + 1):
                        act.wait_ge(p_used, n - PBUF + 1)
                    nc.scalar.activation(prob[s % PBUF][:, 0:width], S[s % 2][:, 0:width],
                                         ACT.Exp).then_inc(p_ready, 1)
                if s == 1 and prepares:
                    act.wait_ge(ln_x[0], b + 2)
                    if due(NS * b):
                        act.wait_ge(p_used, NS * b)
                    nc.scalar.activation(Xs[1 - par][:, :, 0:D], xn[0][:, :, :], ACT.Copy).then_inc(ln_h[0], 1)
                if s == 3 and before:
                    act.wait_ge(ln_xc[1], b)
                    nc.scalar.activation(sq[:, :, :], xn[1][:, :, :], ACT.Square).then_inc(ln_sq[1], 1)
                if s == 6 and before:
                    act.wait_ge(ln_x[1], b)
                    nc.scalar.activation(X2s[:, :, 0:D], xn[1][:, :, :], ACT.Copy).then_inc(ln_h[1], 1)
                if s == 13 and looks:
                    act.wait_ge(ln_xc[0], b + 3)
                    nc.scalar.activation(sq[:, :, :], xn[0][:, :, :], ACT.Square).then_inc(ln_sq[0], 1)
                for point in range(2):
                    if point == 1 and (before if s == 0 else attends) and (s - 1) % NS in LAST:
                        last = (s - 1) % NS
                        act.wait_ge(p_used, NS * b + s if s else NS * b)
                        nc.scalar.activation(YS[:, :], Y[:, :], ACT.Copy).then_inc(y_free, 1)
                    for (ev, pt, k, c) in T_EVENTS:
                        tail = ev - NS == s and attends
                        if pt != point or not (ev == s and prepares or tail):
                            continue
                        nb, q = (b, par) if tail else (b + 1, 1 - par)
                        act.wait_ge(t_full, t_at(k, c, nb) + 1)
                        cols = slice(QB * c, QB * c + QB)
                        if k == "xT":
                            ins = nc.scalar.activation(XT[:, :], T[:, :], ACT.Copy)
                        if k == "proj":
                            ins = nc.scalar.activation(QK[:, :, :].rearrange("p t n -> p (t n)"), T[:, :], ACT.Copy)
                        if k == "kT":
                            ins = nc.scalar.activation(K1[q][:, cols], T[:, :], ACT.Copy)
                        if k == "qT":
                            if due(64 * (2 * nb + (c + 1) // 2)):
                                act.wait_ge(dup[(c + 1) % 2], 64 * (2 * nb + (c + 1) // 2))
                            ins = nc.scalar.activation(QT[:, :], T[:, :], ACT.Copy)
                        if k == "mT":
                            if due(16 * (4 * nb + c)):
                                act.wait_ge(mrow_in, 16 * (4 * nb + c))
                            ins = nc.scalar.activation(mrow[:, :], T[0:TPB, 0:P], ACT.Copy, scale=-1.0)
                        ins.then_inc(t_free, 1)
                    for (ev, pt, k, c) in F_EVENTS:
                        if pt != point or ev != s or not before or k in ("attn", "out"):
                            continue
                        act.wait_ge(f_full, f_at(k, c, b) + 1)
                        if k == "x2T":
                            ins = nc.scalar.activation(X2T[:, :], F[:, :], ACT.Copy)
                        if k == "in":
                            ins = relu(hid[0][:, :], F[:, :], bi_sb[:, 0:1])
                        if k in ("mlp0", "mlp1"):
                            layer = int(k[3])
                            for r in range(2):
                                ins = relu(hid[layer + 1][:, ROUTED * r:ROUTED * r + ROUTED],
                                           F[:, ROUTED * r:ROUTED * r + ROUTED],
                                           wexp[c % 2][:, r, 2 * HID + layer:2 * HID + layer + 1])
                        ins.then_inc(f_free, 1)
            run(act, prologue, step)

        @block.tensor
        def _(pe):
            def prologue():
                pe.wait_ge(load, 16 * 3)
                pe.wait_ge(ready, 2)
                nc.tensor.transpose(T[:, 0:P], ids_f[:, 0, :], ident)
                nc.tensor.matmul(T[:, P:P + D], sm[:, 0:P], sm[:, 256:320], start=True, stop=True)
                nc.tensor.matmul(T[:, P + D:2 * P], sm[:, P:2 * P], sm[:, 320:384], start=True, stop=True)
                nc.tensor.matmul(T[:, 2 * P:2 * P + D], smc[:, :], sm[:, 384:448], start=True,
                                 stop=True).then_inc(folded, 1)
                pe.wait_ge(ready, 4)

            def scores(b, par, s):
                n = NS * b + s
                i, parts = CHUNKS[s]
                if due(n - 1):
                    pe.wait_ge(p_ready, n - 1)
                if s == 0:
                    for d in dup:
                        pe.wait_ge(d, 128 * (b + 1))
                    pe.wait_ge(mrow_in, 16 * (4 * b + 2))
                if s == LAST[1] + 1:
                    pe.wait_ge(mrow_in, 16 * (4 * b + 3))
                if s == LAST[2] + 1:
                    pe.wait_ge(mrow_in, 16 * (4 * b + 4))
                for kt, q0, w, col, mask in parts:
                    dst = S[s % 2][:, col:col + w]
                    qs = slice(QB * i + q0, QB * i + q0 + w)
                    ks = slice(P * kt, P * kt + P)
                    nc.tensor.matmul(dst, K1[par][:, ks], Q1[par][:, qs], start=True, stop=False)
                    ins = nc.tensor.matmul(dst, K2[par][:, ks], Q2[par][:, qs], start=False, stop=not mask)
                    if mask == "edge":
                        ins = nc.tensor.matmul(dst[:, 0:P], identb, edge, start=False, stop=True)
                    if mask == "full+edge":
                        ins = nc.tensor.matmul(dst, identb, full_edge, start=False, stop=True)
                ins.then_inc(s_full, 1)

            def values(b, par, s):
                i, parts = CHUNKS[s]
                first = s == 0 or CHUNKS[s - 1][0] != i
                pe.wait_ge(p_ready, NS * b + s + 1)
                if s == 0:
                    pe.wait_ge(ones_in, b + 1)
                if first:
                    if due(4 * b + i):
                        pe.wait_ge(y_free, 4 * b + i)
                for n, (kt, q0, w, col, _) in enumerate(parts):
                    last = s in LAST and n == len(parts) - 1
                    ins = nc.tensor.matmul(Y[:, q0:q0 + w], Xs[par][:, kt, :].bitcast(F32),
                                           prob[s % PBUF][:, col:col + w],
                                           start=first and n == 0, stop=last)
                ins.then_inc(p_used, 1)

            def turn(k, c, nb, q):
                at = t_at(k, c, nb)
                if due(at):
                    pe.wait_ge(t_free, at)
                for j in range(TPB):
                    t = TPB * c + j
                    dst = T[:, P * j:P * j + P]
                    if k == "xT":
                        if j == 0 and c == 0:
                            pe.wait_ge(ln_l[0], nb + 1)
                        ins = nc.tensor.transpose(dst, Xs[q][:, t, :].bitcast(F32), ident)
                    if k == "proj":
                        if j == 0:
                            pe.wait_ge(t_free, t_at("xT", c, nb) + 1)
                        ins = nc.tensor.matmul(dst, XT[:, P * j:P * j + P], wqk[:, :], start=True, stop=True)
                    if k == "kT":
                        if j == 0:
                            pe.wait_ge(split, 4 * nb + c + 1)
                        ins = nc.tensor.transpose(dst, QKs[:, j, 2 * D:4 * D].bitcast(F32), ident)
                    if k == "qT":
                        ins = nc.tensor.transpose(dst, QKs[:, j, 0:2 * D].bitcast(F32), ident)
                if k == "mT":
                    pe.wait_ge(nm_ready, 4 * nb + c + 1)
                    ins = nc.tensor.transpose(T[0:TPB, 0:P], nm[c % 2][:, :], ident)
                ins.then_inc(t_full, 1)

            def piece(n, nb, q):
                t, g = PIECES[n]
                c = t // TPB
                if t % TPB == 0 and g == 0:
                    pe.wait_ge(dup[c % 2], 64 * (2 * nb + c // 2 + 1))
                if due(NM * nb + n):
                    pe.wait_ge(m_free, NM * nb + n)
                w = min(QB, P * (t + 1) - QB * g)
                last = g == c
                nc_w = max(w, 2 * P)
                ins = nc.tensor.matmul(M[:, 0:nc_w], Q1[q][:, P * t:P * t + P],
                                       K1[q][:, QB * g:QB * g + nc_w], start=True, stop=not last)
                if last:
                    ins = nc.tensor.matmul(M[:, w - P:w], identb, edge_q, start=False, stop=True)
                ins.then_inc(m_full, 1)

            def mlp(k, c, b):
                if due(f_at(k, c, b)):
                    pe.wait_ge(f_free, f_at(k, c, b))
                if k == "attn":
                    pe.wait_ge(y_free, 4 * b + c + 1 if c < 3 else 4 * b)
                    for j in range(TPB):
                        ins = nc.tensor.matmul(F[:, P * j:P * j + P], YS[:, P * j:P * j + P], wv[:, :],
                                               start=True, stop=True)
                if k == "x2T":
                    if c == 0:
                        pe.wait_ge(ln_l[1], b)
                    for j in range(TPB):
                        ins = nc.tensor.transpose(F[:, P * j:P * j + P], X2s[:, TPB * c + j, :].bitcast(F32), ident)
                if k == "in":
                    pe.wait_ge(f_free, f_at("x2T", c, b) + 1)
                    nc.tensor.matmul(F[:, :], wi_h[:, :], X2T[:, :], start=True, stop=False)
                    ins = nc.tensor.matmul(F[:, :], wi_l[:, :], X2T[:, :], start=False, stop=True)
                if k in ("mlp0", "mlp1"):
                    layer = int(k[3])
                    pe.wait_ge(f_free, f_at("in" if layer == 0 else "mlp0", c, b) + 1)
                    if layer == 0:
                        pe.wait_ge(w_in[c % 2], 32 * (2 * (b - 1) + c // 2 + 1))
                    for r in range(2):
                        cols = slice(ROUTED * r, ROUTED * r + ROUTED)
                        ins = nc.tensor.matmul(F[:, cols], wexp[c % 2][:, r, HID * layer:HID * layer + HID],
                                               hid[layer][:, cols], start=True, stop=True)
                if k == "out":
                    pe.wait_ge(f_free, f_at("mlp1", c, b) + 1)
                    for j in range(TPB):
                        ins = nc.tensor.matmul(F[:, P * j:P * j + WOW], hid[2][:, P * j:P * j + P],
                                               wo_sb[:, :], start=True, stop=True)
                ins.then_inc(f_full, 1)

            def step(b, par, s):
                attends, before, prepares, _ = on(b)
                if attends:
                    scores(b, par, s)
                todo = [(n, b + 1, 1 - par) for n in piece_at(s, 0)] if prepares else []
                todo += [(n, b, par) for n in piece_at(s, 1)] if attends else []
                half = (len(todo) + 1) // 2
                for point in range(2):
                    if point == 1:
                        if s > 0 and attends:
                            values(b, par, s - 1)
                        if s == 0 and before:
                            values(b - 1, 1 - par, NS - 1)
                    now = todo[half:] if point else todo[:half]
                    if now:
                        piece(*now.pop(0))
                    for (ev, pt, k, c) in T_EVENTS:
                        if pt == point and ev == s and prepares:
                            turn(k, c, b + 1, 1 - par)
                        if pt == point and ev - NS == s and attends:
                            turn(k, c, b, par)
                    if now:
                        piece(*now.pop(0))
                    for (ev, pt, k, c) in F_EVENTS:
                        if pt == point and ev == s and (attends if k == "attn" and c < 3 else before):
                            mlp(k, c, b)
            run(pe, prologue, step)

        @block.vector
        def _(dve):
            def prologue():
                v = nc.vector
                v.memset(wo_sb[:, :], 0.0).then_inc(ready, 1)
                v.memset(wv[:, :], 0.0)
                for n in range(2):
                    v.memset(O[n][:, :, :], 0.0).then_inc(out_dma[n], 16)
                v.memset(rows_all[:, P:P + TILES].bitcast(F32), 0.0)
                for n in range(2):
                    for q in (K2[n], Q2[n]):
                        v.memset(q[D:P, :].bitcast(F32), 0.0)
                v.drain()
                for n in range(2):
                    v.memset(K2[n][D:D + 1, :].bitcast(F32), 1.0)
                dve.wait_ge(load, 16 * 3)
                v.tensor_copy(ids_f[:, 0, :], ids_i[:, :])
                v.drain()
                v.tensor_scalar(ids_f[:, 1, :], ids_f[:, 0, :], 0.0, float(VOCAB), ALU.is_lt, ALU.mult)
                v.drain()
                v.tensor_tensor(ids_f[:, 0, :], ids_f[:, 0, :], ids_f[:, 1, :], ALU.add)
                v.drain()
                v.tensor_scalar(ids_f[:, 0, :], ids_f[:, 0, :], 0.0, float(VOCAB - 1), ALU.max, ALU.min)
                v.drain()
                v.tensor_scalar(ids_f[:, 0, :], ids_f[:, 0, :], float(HIDDEN // D), float(SLICE), ALU.mult, ALU.add)
                v.tensor_copy(conb[:, :], con[:, :])
                v.tensor_scalar(smc[:, 0:D], sm[:, P:P + D], sm[:, P + D - 1:P + D], None, ALU.subtract)
                v.drain()
                v.tensor_copy(smc[:, D:P], smc[:, 0:D]).then_inc(ready, 1)
            def prologue2():
                v = nc.vector
                dve.wait_ge(folded, 1)
                dve.wait_ge(load2, 16 * 10)
                v.tensor_copy(rows_all[:, 0:P], T[:, 0:P])
                v.tensor_scalar(wqk[:, 0:D], T[:, P:P + D], D ** -0.5, None, ALU.mult)
                v.tensor_copy(wqk[:, D:P], T[:, P + D:2 * P])
                v.tensor_copy(wv[:, 0:D], T[:, 2 * P:2 * P + D])
                v.tensor_copy(wv[:, D:D + 1], ident[:, D - 1:D])
                v.tensor_copy(wi_h[:, :], wi_sb[:, :])
                v.drain()
                v.tensor_tensor(wi_l[:, :], wi_sb[:, :], wi_h[:, :].bitcast(F32), ALU.subtract)
                for layer in range(N_LAYERS):
                    w = experts[:, N_EXPERTS, HID * layer:HID * layer + HID]
                    v.tensor_tensor(w, w, ident, ALU.add)
                v.drain()
                v.tensor_tensor(experts[:, 0:N_EXPERTS, :], experts[:, 0:N_EXPERTS, :],
                                experts[:, N_EXPERTS:N_EXPERTS + 1, :].broadcast_to([P, N_EXPERTS, EW]), ALU.add)
                v.tensor_copy(route_f[:, 0], route_i[:, :])
                v.drain()
                v.tensor_scalar(route_f[:, 1], route_f[:, 0], 0.0, None, ALU.is_ge)
                v.tensor_scalar(route_f[:, 2], route_f[:, 0], float(N_EXPERTS - 1), None, ALU.is_le)
                v.drain()
                v.tensor_tensor(route_f[:, 1], route_f[:, 1], route_f[:, 2], ALU.mult)
                v.tensor_scalar(route_f[:, 0], route_f[:, 0], -1.0, float(N_EXPERTS), ALU.max, ALU.min)
                v.drain()
                v.tensor_scalar(route_f[:, 0], route_f[:, 0], float(-N_EXPERTS), None, ALU.add)
                v.drain()
                v.tensor_tensor(route_f[:, 0], route_f[:, 0], route_f[:, 1], ALU.mult)
                v.drain()
                v.tensor_scalar(route_e[:, :], route_f[:, 0], float(N_EXPERTS), None, ALU.add)
                v.drain()
                v.tensor_copy(rec[:, 0:1], bi_sb[:, :]).then_inc(ready, 2)

            def sums(n, which, src):
                nc.vector.tensor_reduce(stat[n][:, 2 * which, :], src, AX.X, ALU.add).then_inc(
                    (ln_sum if which == 0 else ln_var)[n], 1)

            def reduce_piece(n, nb):
                t, g = PIECES[n]
                c = t // TPB
                w = min(QB, P * (t + 1) - QB * g)
                dve.wait_ge(m_full, NM * nb + n + 1)
                nc.vector.tensor_reduce(pm[c % 2][:, t % TPB, g:g + 1], M[:, 0:w], AX.X, ALU.max).then_inc(m_free, 1)
                if t % TPB == TPB - 1 and g == c:
                    nc.vector.drain()
                    nc.vector.tensor_reduce(nm[c % 2][:, :], pm[c % 2][:, :, 0:c + 1], AX.X, ALU.max).then_inc(nm_ready, 1)
                    nc.vector.drain()

            def step(b, par, s):
                v = nc.vector
                attends, before, prepares, looks = on(b)
                if s == 0 and looks:
                    if due(256 * (b + 2)):
                        dve.wait_ge(gathered, 256 * (b + 2))
                    v.tensor_copy(rows_now[:, :], rows_all[:, bass.ds(TILES * (b + 2), TILES)]).then_inc(rows_ready, 1)
                if s == 2 and before:
                    v.drain()
                    sums(1, 0, H1[1 - par][:, :, :])
                if s == 5 and before:
                    dve.wait_ge(ln_sq[1], b)
                    sums(1, 1, sq[:, :, :])
                if s == 12 and looks:
                    dve.wait_ge(gathered, 256 * (b + 3))
                    sums(0, 0, G[par][:, :, :])
                if s == 15 and looks:
                    dve.wait_ge(ln_sq[0], b + 3)
                    sums(0, 1, sq[:, :, :])
                todo = [(n, b + 1) for n in piece_at(s, 0)] if prepares else []
                todo += [(n, b) for n in piece_at(s, 1)] if attends else []
                half = (len(todo) + 1) // 2
                for point in range(2):
                    for one in (todo[half:] if point else todo[:half]):
                        reduce_piece(*one)
                    for (ev, pt, k, c) in T_EVENTS:
                        if point == 0 or ev != s or not prepares:
                            continue
                        if k == "proj":
                            dve.wait_ge(roped, 4 * (b + 1) + c + 1)
                            if c > 0:
                                dve.wait_ge(t_full, t_at("qT", c - 1, b + 1) + 1)
                            v.tensor_copy(QKs[:, :, D:3 * D], QK[:, :, :])
                            v.drain()
                            low = QKs[:, :, :].rearrange("p t (f d) -> p t f d", f=4)[:, :, 0:4:3, :]
                            high = QKs[:, :, D:3 * D].rearrange("p t (a d) -> p t a d", a=2)
                            v.tensor_tensor(low, QK[:, :, :].rearrange("p t (a d) -> p t a d", a=2),
                                            high.bitcast(F32), ALU.subtract).then_inc(split, 1)
                        if k == "qT" and c == 3:
                            dve.wait_ge(t_full, t_at("xT", 3, b + 1) + 1)
                            v.memset(Xs[1 - par][:, :, D - 1:D].bitcast(F32), 1.0)
                            v.memset(Xs[1 - par][:, :, P - 1:P].bitcast(F32), 0.0).then_inc(ones_in, 1)
                    for (ev, pt, k, c) in F_EVENTS:
                        if pt != point or ev != s:
                            continue
                        if k == "attn" and (attends if c < 3 else before):
                            hb, q = (b, par) if c < 3 else (b - 1, 1 - par)
                            tiles = slice(TPB * c, TPB * c + TPB)
                            dve.wait_ge(f_full, f_at(k, c, b) + 1)
                            dve.wait_ge(hres_in, 16 * (hb + 1))
                            f = F[:, :].rearrange("p (t n) -> p t n", n=P)
                            v.reciprocal(rec[:, :].unsqueeze(2), f[:, :, D:D + 1])
                            v.drain()
                            v.tensor_tensor(att[:, :, :], f[:, :, 0:D], rec[:, :].unsqueeze(2).broadcast_to([P, TPB, D]),
                                            ALU.mult).then_inc(f_free, 1)
                            v.drain()
                            v.tensor_tensor(H1[q][:, tiles, :], att[:, :, :], Hres[q][:, tiles, :],
                                            ALU.add).then_inc(h1_done, 1)
                        if k == "out" and before:
                            dve.wait_ge(f_full, f_at(k, c, b) + 1)
                            dve.wait_ge(h1b_ready, b)
                            dve.wait_ge(out_dma[c % 2], 16 * (2 * (b - 1) + c // 2 + 1))
                            f = F[:, :].rearrange("p (t n) -> p t n", n=P)
                            v.tensor_tensor(O[c % 2][:, :, :], f[:, :, 0:D], H1b[:, TPB * c:TPB * c + TPB, :],
                                            ALU.add).then_inc(f_free, 1)

            def first():
                prologue()
                prologue2()
            run(dve, first, step)


_DTYPES = {"float32": F32, "int32": I32}


def shape_constants():
    k, q = np.arange(P)[:, None], np.arange(P)[None, :]
    edge = np.where(k > q, np.float32(NEG), np.float32(0))
    full = np.full((P, P), NEG, np.float32)
    consts = np.concatenate([np.eye(P, dtype=np.float32), full, edge, edge.T], axis=1)
    half = ROPE // 2
    theta = np.float32(1.0) / np.float32(10000.0) ** (np.arange(half, dtype=np.float32) / np.float32(half))
    angle = (np.arange(SEQ, dtype=np.float32)[:, None] * theta[None, :]).astype(np.float32)
    sin, cos = np.sin(angle), np.cos(angle)
    cos2 = np.repeat(cos, 2, axis=1)
    sin2 = np.stack([-sin, sin], axis=-1).reshape(SEQ, ROPE)
    tabs = np.stack([cos2, sin2]).reshape(2, TILES, P, 1, ROPE)
    tabs = np.broadcast_to(tabs, (2, TILES, P, 2, ROPE)).transpose(2, 0, 1, 3, 4)
    return np.ascontiguousarray(consts, np.float32), np.ascontiguousarray(tabs, np.float32)


def kernel(**inputs):
    import concourse.bacc as _bacc
    from concourse.bass_utils import run_bass_kernel_spmd as _run

    a = {k: np.asarray(v) for k, v in inputs.items()}
    at, ff = "L0_attn_", "L0_ffn_"
    consts, rope = shape_constants()
    wq, wkv = a[at + "Wq_comp"].T, a[at + "Wkv_comp"].T
    small = np.concatenate([wq, wq, wkv, wkv, a[at + "Wqc"], a[at + "Wqr"], a[at + "Wkc"], a[at + "Wkr"],
                            a[at + "Wv"]], axis=1)
    wit = a[ff + "Wi"].T
    arrays = {
        "ids": a["x"].reshape(P, P),
        "table": a["L0_tok_ple_table"],
        "consts": consts,
        "rope": rope,
        "small": small,
        "wi": np.concatenate([wit, wit], axis=0),
        "wo": a[ff + "Wo"].T,
        "wr": a[ff + "Wr"].transpose(3, 1, 0, 2).reshape(P, N_EXPERTS, N_LAYERS * HID),
        "ws": a[ff + "Ws"][:, 0].transpose(2, 0, 1).reshape(P, N_LAYERS * HID),
        "brt": a[ff + "br"].transpose(2, 1, 0),
        "bst": a[ff + "bs"][:, 0].T,
        "bi": a[ff + "bi"].reshape(P, 1),
        "bo": np.broadcast_to(a[ff + "bo"], (P, D)),
        "route": a[ff + "route_id"].reshape(1, 64),
    }
    nc = _bacc.Bacc("TRN2", target_bir_lowering=False, num_devices=1)
    feeds, args = {}, []
    for name, v in arrays.items():
        v = np.ascontiguousarray(v)
        feeds[f"in_{name}"] = v
        args.append(nc.dram_tensor(f"in_{name}", v.shape, _DTYPES[v.dtype.name], kind="ExternalInput").ap())
    args.append(nc.dram_tensor("out_0", (BATCH, SEQ, D), F32, kind="ExternalOutput").ap())
    tower_kernel(nc, *args)
    r = _run(nc, [feeds], core_ids=[0])
    return r.results[0]["out_0"]
```

```python
from contextlib import ExitStack

import concourse.bass as bass
import numpy as np
from concourse import mybir
from concourse.alu_op_type import AluOpType as ALU

ACT = mybir.ActivationFunctionType
AX = mybir.AxisListType
F32 = mybir.dt.float32
F32R = mybir.dt.float32r
BF16 = mybir.dt.bfloat16
I32 = mybir.dt.int32

P = 128
D = 64
BATCH, SEQ = 8, 2048
VOCAB, HIDDEN = 32000, 512
SLICE = 3
ROPE = 16
HID, N_LAYERS, N_EXPERTS = 128, 2, 16
ROUTED = BATCH * SEQ // 64
EPS = 1e-5

TILES = SEQ // P
QB = 512
BLOCKS = SEQ // QB
TPB = QB // P
EW = N_LAYERS * HID + N_LAYERS
WOW = 96
NEG = -1e30


def attention_chunks():
    chunks = []
    for i in range(BLOCKS):
        for kt in range(0, TPB * i, 2):
            chunks.append((i, [(kt, 0, QB, 0, ""), (kt + 1, 0, QB, QB, "")]))
        k = TPB * i
        chunks.append((i, [(k, 0, 512, 0, "edge"), (k + 1, 128, 384, 512, "edge")]))
        chunks.append((i, [(k + 2, 256, 256, 0, "edge"), (k + 3, 256, 256, 256, "full+edge")]))
    return chunks


CHUNKS = attention_chunks()
NS = len(CHUNKS)
LAST = [max(n for n, ch in enumerate(CHUNKS) if ch[0] == i) for i in range(BLOCKS)]
PBUF = 3
DVE_ALONE = (5, 6)
LAG = 2


def max_pieces():
    return [(t, g) for t in range(TILES) for g in range(t // TPB + 1)]


PIECES = max_pieces()
NM = len(PIECES)

T_EVENTS = sorted(
    [(3 * c + 4, 0, "xT", c) for c in range(BLOCKS)]
    + [(3 * c + 5, 0, "proj", c) for c in range(BLOCKS)]
    + [(3 * c + 7, 1, "kT", c) for c in range(BLOCKS)]
    + [(3 * c + 8, 1, "qT", c) for c in range(BLOCKS)]
    + [(s, 1, "mT", c) for c, s in enumerate((12, 16, NS + 2, NS + 10))]
)
NT = len(T_EVENTS)
T_FIRST = sorted([e for e in T_EVENTS if e[2] != "mT"] + [(15, 1, "mT", 0), (18, 1, "mT", 1)])
T_ORDER = [(k, c) for _, _, _, k, c in sorted((s % NS, pt, s >= NS, k, c) for s, pt, k, c in T_EVENTS)]
T_TAIL = [(k, c) for s, _, k, c in T_EVENTS if s >= NS]
MAX_AT = {10: 2, 11: 2, 13: 2, 14: 3, 15: 3}
MAX_AT.update({s: 2 for s in range(16, NS + 10)})
MAX_FIRST = {13: 2, 14: 2, 16: 4, 17: 4, 18: 4, 19: 4}
assert sum(MAX_FIRST.values()) == sum(n for s, n in MAX_AT.items() if s < NS)
F_EVENTS = sorted(
    [(h // 2, h % 2, "attn", i) for i, h in enumerate((8, 16, 2, 4))]
    + [(min(h + 2 * j, 2 * NS - 1) // 2, min(h + 2 * j, 2 * NS - 1) % 2, k, c) for c, h in enumerate((19, 22, 29, 32))
       for j, k in enumerate(("x2T", "in", "mlp0", "mlp1", "out"))])
NF = len(F_EVENTS)
USES = ("x2T", "in", "mlp0", "mlp1", "out")
F_LAST = [(1, 0, "attn", 2), (2, 0, "attn", 3)] + [(9 + 2 * j, 0, k, c) for j, k in enumerate(USES)
                                                  for c in range(BLOCKS)]
NF0 = 2
F_ORD = {(k, c): n for n, (_, _, k, c) in enumerate(F_EVENTS)}
F_ORD0 = {("attn", i): i for i in range(NF0)}


def tower_kernel(nc, ids, table, consts, rope, small, wi, wo, wr, ws, brt, bst, bi, bo, route, out):
    table_rows = table.rearrange("v (s d) -> (v s) d", d=D)
    out_v = out.rearrange("b (t p) d -> b p t d", p=P)

    with ExitStack() as ctx:
        def sb(name, shape, dt=F32):
            return ctx.enter_context(nc.sbuf_tensor(name, shape, dt))

        def bank(name, n=1):
            return ctx.enter_context(nc.psum_tensor(name, [P, 512 * n], F32))

        def sem(name):
            return ctx.enter_context(nc.semaphore(name))

        ident = sb("ident", [P, P])[:, :]
        conb = sb("conb", [P, 4 * P], BF16)
        identb, full_edge, edge, edge_q = conb[:, 0:P], conb[:, P:3 * P], conb[:, 2 * P:3 * P], conb[:, 3 * P:4 * P]
        rope_sb = sb("rope_sb", [P, 2, TILES, 2, ROPE])
        wqk = sb("wqk", [P, P])
        wv = sb("wv", [P, P])
        wi_sb = sb("wi_sb", [P, HID])
        wi_h = sb("wi_h", [P, HID], F32R)
        wi_l = sb("wi_l", [P, HID], F32R)
        wo_sb = sb("wo_sb", [P, WOW])
        experts = sb("experts", [P, N_EXPERTS + 1, EW])
        bi_sb = sb("bi_sb", [P, 1])
        bo_sb = sb("bo_sb", [P, D])
        route_i = sb("route_i", [1, 64], I32)
        route_f = sb("route_f", [1, 3, 64])
        route_e = sb("route_e", [1, 64], I32)
        rows_all = sb("rows_all", [P, P + TILES], I32)
        rows_now = sb("rows_now", [P, TILES], I32)
        gate = sb("gate", [P, 1])
        lnc = sb("lnc", [P, 3])
        G = [sb(f"G{n}", [P, TILES, D]) for n in range(2)]
        xn = [sb(f"xn{n}", [P, TILES, D]) for n in range(2)]
        stat = [sb(f"stat{n}", [P, 6, TILES]) for n in range(2)]
        Xs = [sb(f"Xs{n}", [P, TILES, P], F32R) for n in range(2)]
        XT = sb("XT", [P, QB])
        QK = sb("QK", [P, TPB, P])
        rt = sb("rt", [P, 2, TPB, 2, ROPE])
        QKs = sb("QKs", [P, TPB, 4 * D], F32R)
        QT = sb("QT", [P, QB], F32R)
        K1 = [sb(f"K1{n}", [P, SEQ], F32R) for n in range(2)]
        K2 = [sb(f"K2{n}", [P, SEQ], F32R) for n in range(2)]
        Q1 = [sb(f"Q1{n}", [P, SEQ], F32R) for n in range(2)]
        Q2 = [sb(f"Q2{n}", [P, SEQ], F32R) for n in range(2)]
        pm = [sb(f"pm{n}", [P, TPB, BLOCKS]) for n in range(2)]
        nm = [sb(f"nm{n}", [P, TPB]) for n in range(2)]
        mrow = sb("mrow", [TPB, P], F32R)
        prob_h = [sb(f"prob_h{n}", [P, 1024], F32R) for n in range(PBUF)]
        prob_l = [sb(f"prob_l{n}", [P, 1024], F32R) for n in range(PBUF)]
        prob = [sb(f"prob{n}", [P, 1024]) for n in range(2)]
        con = prob[0][:, 0:3 * P]
        sm = prob[1][0:D, 0:448]
        smc = prob[1][0:D, QB:QB + P]
        ids_i = prob[0][:, 3 * P:4 * P].bitcast(I32)
        ids_f = prob[0][:, 4 * P:6 * P].rearrange("p (n t) -> p n t", n=2)
        YS = sb("YS", [P, QB])
        rec = sb("rec", [P, TPB])
        att = sb("att", [P, TPB, D])
        H1 = [sb(f"H1{n}", [P, TILES, D]) for n in range(2)]
        H1b = sb("H1b", [P, TILES, D])
        X2s = sb("X2s", [P, TILES, P], F32R)
        X2T = sb("X2T", [P, QB], F32R)
        hid = [sb(f"hid{n}", [P, QB]) for n in range(2)]
        wexp = [sb(f"wexp{n}", [P, 2, EW]) for n in range(2)]
        O = [sb(f"O{n}", [P, TPB, D]) for n in range(2)]

        S = [bank(f"S{n}", 2) for n in range(2)]
        Y = bank("Y")
        M = bank("M")
        T = bank("T")
        F = bank("F")

        ids_in = sem("ids_in")
        load = sem("load")
        load2 = sem("load2")
        ready = sem("ready")
        folded = sem("folded")
        rows_ready = sem("rows_ready")
        gathered = sem("gathered")
        hres_in = sem("hres_in")
        ln_sum = [sem(f"ln_sum{n}") for n in range(2)]
        ln_xc = [sem(f"ln_xc{n}") for n in range(2)]
        ln_var = [sem(f"ln_var{n}") for n in range(2)]
        ln_sq = [sem(f"ln_sq{n}") for n in range(2)]
        ln_x = [sem(f"ln_x{n}") for n in range(2)]
        ln_h = [sem(f"ln_h{n}") for n in range(2)]
        ln_l = [sem(f"ln_l{n}") for n in range(2)]
        ones_in = sem("ones_in")
        turned = sem("turned")
        roped = sem("roped")
        split = sem("split")
        dup = [sem(f"dup{n}") for n in range(2)]
        mrow_in = sem("mrow_in")
        nm_ready = sem("nm_ready")
        s_full = sem("s_full")
        ph_ready, p_ready = sem("ph_ready"), sem("p_ready")
        pl_dve, pl_pool = sem("pl_dve"), sem("pl_pool")
        p_used = sem("p_used")
        y_free = sem("y_free")
        m_full, m_free = sem("m_full"), sem("m_free")
        t_full, t_free = sem("t_full"), sem("t_free")
        f_full, f_free = sem("f_full"), sem("f_free")
        o_free = sem("o_free")
        h1_done = sem("h1_done")
        h1b_ready = sem("h1b_ready")
        w_in = [sem(f"w_in{n}") for n in range(2)]
        out_dma = [sem(f"out_dma{n}") for n in range(2)]

        def due(n):
            return not isinstance(n, int) or n > 0

        def t_at(k, c, b):
            tail = (k, c) in T_TAIL
            if isinstance(b, int) and b == 0 and not tail:
                return [(k_, c_) for _, _, k_, c_ in T_FIRST].index((k, c))
            n = T_ORDER.index((k, c))
            if isinstance(b, int) and b == BATCH - 1 and tail:
                n = T_TAIL.index((k, c))
            return NT * (b + tail) - len(T_TAIL) + n

        def t_events(it):
            return T_FIRST if isinstance(it, int) and it == -1 else T_EVENTS

        def is_last(it):
            return isinstance(it, int) and it == BATCH

        def f_events(it):
            return F_LAST if is_last(it) else F_EVENTS

        def mlp_buffers(c, it):
            if not is_last(it):
                return F[:, :], X2T[:, :], hid[c % 2][:, :], wexp[c % 2][:, :, :]
            cols = slice(QB * (c % 2), QB * (c % 2) + QB)
            w = wexp[c][:, :, :] if c < 2 else G[c - 2][:, :, :].rearrange("p t d -> p (t d)")[
                :, 0:2 * EW].rearrange("p (r n) -> p r n", r=2)
            return S[c // 2][:, cols], prob_h[c // 2][:, cols], prob[c // 2][:, cols], w

        def f_at(k, c, it):
            if isinstance(it, int) and it == 0:
                return F_ORD0[k, c]
            n = [(k_, c_) for _, _, k_, c_ in f_events(it)].index((k, c))
            return NF * it + (NF0 - NF) + n

        def piece_at(table, s):
            first = sum(n for x, n in table.items() if x < s)
            return list(range(first, first + table.get(s, 0)))

        def pieces(b, s):
            attends, _, prepares, _ = on(b)
            own = piece_at(MAX_FIRST if isinstance(b, int) and b == -1 else MAX_AT, s)
            return ([(n, b + 1, False) for n in own] if prepares else []) + (
                [(n, b, True) for n in piece_at(MAX_AT, NS + s)] if attends else [])

        first_banks = [M[:, :]] + [S[n][:, QB * m:QB * m + QB] for n in range(2) for m in range(2)]

        def max_bank(n, nb):
            if isinstance(nb, int) and nb == 0 and n < sum(MAX_FIRST.values()):
                return first_banks[n % 5], 5
            return M[:, :], 1

        def lagging(b, par, s, lag):
            return (b, par, s - lag) if s >= lag else (b - 1, 1 - par, s - lag + NS)

        def exists(b):
            return not isinstance(b, int) or 0 <= b < BATCH

        def cut(s):
            _, parts = CHUNKS[s]
            width = parts[-1][3] + parts[-1][2]
            return width, width if s in DVE_ALONE else width * 5 // 8

        def by_pool(b, s):
            return (NS - len(DVE_ALONE)) * b + sum(1 for m in range(s + 1) if m not in DVE_ALONE)

        def iteration(step_of, b, par):
            for s in range(NS):
                step_of(b, par, s)

        def run(eng, prologue, step_of):
            prologue()
            for b in (-2, -1, 0):
                iteration(step_of, b, b % 2)
            with eng.Fori(0, 3) as j:
                iteration(step_of, j * 2 + 1, 1)
                iteration(step_of, j * 2 + 2, 0)
            for b in (7, 8):
                iteration(step_of, b, b % 2)

        def on(b):
            if not isinstance(b, int):
                return True, True, True, True
            return 0 <= b < BATCH, 0 < b <= BATCH, -1 <= b < BATCH - 1, b < BATCH - 2

        block = ctx.enter_context(nc.Block())

        @block.sync
        def _(sp):
            def prologue():
                sp.dma_start(ids_i, ids).then_inc(ids_in, 16)
                sp.dma_start(ident, consts[:, 0:P]).then_inc(load, 16)
                sp.dma_start(con, consts[:, P:4 * P]).then_inc(load, 16)
                sp.dma_start(sm, small).then_inc(load, 16)
                sp.dma_start(rope_sb[:, :, :, :, :], rope).then_inc(load, 16)
                sp.dma_start(wi_sb[:, :], wi).then_inc(load, 16)
                sp.dma_start(route_i[:, :], route).then_inc(load2, 16)
                sp.dma_start(bi_sb[:, :], bi).then_inc(load2, 16)
                sp.dma_start(bo_sb[:, :], bo).then_inc(load2, 16)
                sp.dma_start(experts[:, N_EXPERTS, 0:2 * HID], ws).then_inc(load2, 16)
                sp.dma_start(experts[:, N_EXPERTS, 2 * HID:EW], bst).then_inc(load2, 16)
                sp.dma_start(experts[:, 0:N_EXPERTS, 0:2 * HID], wr).then_inc(load2, 16)
                sp.dma_start(experts[:, 0:N_EXPERTS, 2 * HID:EW], brt).then_inc(load2, 16)
                sp.wait_ge(ready, 1)
                sp.dma_start(wo_sb[:, 0:D], wo).then_inc(load2, 16)

            def step(b, par, s):
                attends, before, prepares, _ = on(b)
                if s == 0 and isinstance(b, int) and b == 0:
                    sp.wait_ge(ready, 4)
                if s == 13 and prepares:
                    if isinstance(b, int):
                        sp.wait_ge(gathered, 256 * (b + 2))
                    if due(b):
                        sp.wait_ge(h1b_ready, b)
                    sp.dma_start(H1[1 - par][:, :, :], G[1 - par][:, :, :]).then_inc(hres_in, 16)
                for (ev, _, k, c) in t_events(b):
                    if ev == s and prepares:
                        nb = b + 1
                        cols = slice(QB * c, QB * c + QB)
                        if k == "kT":
                            sp.wait_ge(t_free, t_at("kT", c, nb) + 1)
                            sp.dma_start(K2[1 - par][0:D, cols].bitcast(F32),
                                         K1[1 - par][0:D, cols].bitcast(F32)).then_inc(dup[c % 2], 16)
                        if k == "qT":
                            sp.wait_ge(t_free, t_at("qT", c, nb) + 1)
                            for dst, src in ((Q1[1 - par][0:D, cols], QT[D:P, :]), (Q1[1 - par][D:P, cols], QT[D:P, :]),
                                             (Q2[1 - par][0:D, cols], QT[0:D, :])):
                                sp.dma_start(dst.bitcast(F32), src.bitcast(F32)).then_inc(dup[c % 2], 16)
                    tail = ev - NS == s and attends
                    if (ev == s and prepares or tail) and k == "mT":
                        nb, q = (b, par) if tail else (b + 1, 1 - par)
                        sp.wait_ge(t_free, t_at("mT", c, nb) + 1)
                        sp.dma_start(Q2[q][D:D + 1, QB * c:QB * c + QB].bitcast(F32),
                                     mrow[:, :].bitcast(F32)).then_inc(mrow_in, 16)
                for (ev, _, k, c) in f_events(b):
                    if k == "x2T" and s == ev - 2 and before:
                        if is_last(b):
                            if c == 2:
                                sp.wait_ge(hres_in, 16 * BATCH)
                        elif c >= 2:
                            sp.wait_ge(f_free, f_at("mlp1", c - 2, b) + 1)
                        for r in range(2):
                            e = sp.value_load(route_e[0:1, bass.ds(8 * (b - 1) + 2 * c + r, 1)],
                                              min_val=0, max_val=N_EXPERTS)
                            sp.dma_start(mlp_buffers(c, b)[3][:, r, :], experts[:, bass.ds(e, 1), :].rearrange(
                                "p a n -> p (a n)")).then_inc(w_in[c % 2], 16)
                    if k == "out" and s == ev and before:
                        if is_last(b):
                            sp.wait_ge(o_free, c + 1)
                        else:
                            sp.wait_ge(f_free, f_at("out", c, b) + 1)
                        sp.dma_start(out_v[bass.ds(b - 1, 1), :, TPB * c:TPB * c + TPB, :].rearrange(
                            "a p t d -> (a p) t d"), O[c % 2][:, :, :]).then_inc(out_dma[c % 2], 16)

            run(sp, prologue, step)
            for n in range(2):
                sp.wait_ge(out_dma[n], 16 * (2 * BATCH + 1))

        @block.gpsimd
        def _(pool):
            def prologue():
                nc.gpsimd.memset(gate[:, :], 0.0)
                for n, x in enumerate((1.0 / D, EPS, -0.5)):
                    nc.gpsimd.memset(lnc[:, n:n + 1], x)
                nc.gpsimd.drain()

            def centre(n, src):
                p, st = nc.gpsimd, stat[n]
                p.tensor_tensor(st[:, 1, :], st[:, 0, :], lnc[:, 0:1].broadcast_to([P, TILES]), ALU.mult)
                p.drain()
                p.tensor_tensor(xn[n][:, :, :], src, st[:, 1, :].unsqueeze(2).broadcast_to([P, TILES, D]),
                                ALU.subtract).then_inc(ln_xc[n], 1)

            def normalise(n):
                p, st = nc.gpsimd, stat[n]
                for row, op in ((2, ALU.mult), (3, ALU.add), (4, ALU.pow)):
                    p.tensor_tensor(st[:, row + 1, :], st[:, row, :],
                                    lnc[:, row - 2:row - 1].broadcast_to([P, TILES]), op)
                    p.drain()
                p.tensor_tensor(xn[n][:, :, :], xn[n][:, :, :],
                                st[:, 5, :].unsqueeze(2).broadcast_to([P, TILES, D]), ALU.mult).then_inc(ln_x[n], 1)

            def step(b, par, s):
                attends, before, prepares, looks = on(b)
                lb, _, ls = lagging(b, par, s, 1)
                if exists(lb) and ls not in DVE_ALONE:
                    width, w = cut(ls)
                    pool.wait_ge(p_ready, NS * lb + ls + 1)
                    nc.gpsimd.tensor_tensor(prob_l[ls % PBUF][:, w:width], prob[ls % 2][:, w:width],
                                            prob_h[ls % PBUF][:, w:width].bitcast(F32),
                                            ALU.subtract).then_inc(pl_pool, 1)
                if s == 17 and looks:
                    pool.wait_ge(ln_sum[0], b + 3)
                    centre(0, G[par][:, :, :])
                if s == 19 and looks:
                    pool.wait_ge(ln_var[0], b + 3)
                    normalise(0)
                for (ev, _, k, c) in t_events(b):
                    if k == "proj" and ev == s and prepares:
                        nb = b + 1
                        pool.wait_ge(t_free, t_at("proj", c, nb) + 1)
                        r = QK[:, :, :].rearrange("p t (a d) -> p t a d", a=2)[:, :, :, D - ROPE:D]
                        cos, sin = (rope_sb[:, n, TPB * c:TPB * c + TPB] for n in range(2))
                        for half in range(2):
                            nc.gpsimd.tensor_tensor(rt[:, 1, :, :, half::2], r[:, :, :, 1 - half::2],
                                                    sin[:, :, :, half::2], ALU.mult)
                        nc.gpsimd.tensor_tensor(rt[:, 0], r, cos, ALU.mult).then_inc(turned, 1)
                        pool.wait_ge(turned, 4 * nb + c + 1)
                        nc.gpsimd.tensor_tensor(r, rt[:, 0], rt[:, 1], ALU.add).then_inc(roped, 1)
                if s == 2 and before:
                    pool.wait_ge(ln_sum[1], b)
                    centre(1, H1[1 - par][:, :, :])
                if s == 5 and before:
                    pool.wait_ge(ln_var[1], b)
                    normalise(1)
                if s == 1 and looks:
                    pool.wait_ge(rows_ready, b + 3)
                    if due(16 * (b + 1)):
                        pool.wait_ge(hres_in, 16 * (b + 1))
                    nc.gpsimd.tensor_tensor(gate[:, :], gate[:, :], gate[:, :], ALU.mult)
                if 1 <= s <= TILES and looks:
                    nc.gpsimd.indirect_dma_start(
                        out=G[par][:, s - 1, :], out_offset=None, in_=table_rows,
                        in_offset=bass.IndirectOffsetOnAxis(ap=rows_now[:, s - 1:s], axis=0),
                    ).then_inc(gathered, 16)
                if s == 12 and before:
                    pool.wait_ge(h1_done, 4 * b)
                    if not isinstance(b, int) or b > 1:
                        pool.wait_ge(f_free, f_at("out", 3, b - 1) + 1)
                    nc.gpsimd.tensor_tensor(H1b[:, :, :], H1[1 - par][:, :, :],
                                            bo_sb[:, :].unsqueeze(1).broadcast_to([P, TILES, D]),
                                            ALU.add).then_inc(h1b_ready, 1)
            run(pool, prologue, step)

        @block.scalar
        def _(act):
            def prologue():
                pass

            def relu(dst, src, bias):
                return nc.scalar.activation(dst, src, ACT.Relu, bias=bias)

            def step(b, par, s):
                attends, before, prepares, looks = on(b)
                if attends:
                    n = NS * b + s
                    i, parts = CHUNKS[s]
                    width = parts[-1][3] + parts[-1][2]
                    act.wait_ge(s_full, n + 1)
                    same = [m for m in range(NS) if m % PBUF == s % PBUF]
                    used = NS * b + s - PBUF + 1 if s >= PBUF else NS * (b - 1) + same[-1] + 1
                    if due(used):
                        act.wait_ge(p_used, used)
                    nc.scalar.activation(prob_h[s % PBUF][:, 0:width], S[s % 2][:, 0:width],
                                         ACT.Exp).then_inc(ph_ready, 1)
                for point in range(2):
                    if point == 1 and attends:
                        if due(n - 1):
                            act.wait_ge(pl_dve, n - 1)
                            act.wait_ge(pl_pool, by_pool(b, s - 2) if s >= 2 else by_pool(b - 1, s - 2 + NS))
                        nc.scalar.activation(prob[s % 2][:, 0:width], S[s % 2][:, 0:width],
                                             ACT.Exp).then_inc(p_ready, 1)
                    lb, _, ls = lagging(b, par, s, LAG)
                    if point == 1 and exists(lb) and ls in LAST:
                        act.wait_ge(p_used, NS * lb + ls + 1)
                        nc.scalar.activation(YS[:, :], Y[:, :], ACT.Copy).then_inc(y_free, 1)
                    for (ev, pt, k, c) in t_events(b):
                        tail = ev - NS == s and attends
                        if pt != point or not (ev == s and prepares or tail):
                            continue
                        nb, q = (b, par) if tail else (b + 1, 1 - par)
                        act.wait_ge(t_full, t_at(k, c, nb) + 1)
                        cols = slice(QB * c, QB * c + QB)
                        if k == "xT":
                            ins = nc.scalar.activation(XT[:, :], T[:, :], ACT.Copy)
                        if k == "proj":
                            ins = nc.scalar.activation(QK[:, :, :].rearrange("p t n -> p (t n)"), T[:, :], ACT.Copy)
                        if k == "kT":
                            ins = nc.scalar.activation(K1[q][:, cols], T[:, :], ACT.Copy)
                        if k == "qT":
                            if due(64 * (2 * nb + (c + 1) // 2)):
                                act.wait_ge(dup[(c + 1) % 2], 64 * (2 * nb + (c + 1) // 2))
                            ins = nc.scalar.activation(QT[:, :], T[:, :], ACT.Copy)
                        if k == "mT":
                            if due(16 * (4 * nb + c)):
                                act.wait_ge(mrow_in, 16 * (4 * nb + c))
                            ins = nc.scalar.activation(mrow[:, :], T[0:TPB, 0:P], ACT.Copy, scale=-1.0)
                        ins.then_inc(t_free, 1)
                    for (ev, pt, k, c) in f_events(b):
                        if pt != point or ev != s or not before or k in ("attn", "out"):
                            continue
                        act.wait_ge(f_full, f_at(k, c, b) + 1)
                        bank, x2t, h, w = mlp_buffers(c, b)
                        if k == "x2T":
                            ins = nc.scalar.activation(x2t, bank, ACT.Copy)
                        if k == "in":
                            ins = relu(h, bank, bi_sb[:, 0:1])
                        if k in ("mlp0", "mlp1"):
                            layer = int(k[3])
                            for r in range(2):
                                cols = slice(ROUTED * r, ROUTED * r + ROUTED)
                                ins = relu(h[:, cols], bank[:, cols],
                                           w[:, r, 2 * HID + layer:2 * HID + layer + 1])
                        ins.then_inc(f_free, 1)
                if s == 2 and prepares:
                    act.wait_ge(ln_x[0], b + 2)
                    if due(NS * b):
                        act.wait_ge(p_used, NS * b)
                    nc.scalar.activation(Xs[1 - par][:, :, 0:D], xn[0][:, :, :], ACT.Copy).then_inc(ln_h[0], 1)
                if s == 3 and before:
                    act.wait_ge(ln_xc[1], b)
                    act.wait_ge(ln_l[0], b + 2 if prepares else BATCH)
                    nc.scalar.activation(xn[0][:, :, :], xn[1][:, :, :], ACT.Square).then_inc(ln_sq[1], 1)
                if s == 7 and before:
                    act.wait_ge(ln_x[1], b)
                    nc.scalar.activation(X2s[:, :, 0:D], xn[1][:, :, :], ACT.Copy).then_inc(ln_h[1], 1)
                if s == 18 and looks:
                    act.wait_ge(ln_xc[0], b + 3)
                    if due(b):
                        act.wait_ge(ln_l[1], b)
                    nc.scalar.activation(xn[1][:, :, :], xn[0][:, :, :], ACT.Square).then_inc(ln_sq[0], 1)
            run(act, prologue, step)

        @block.tensor
        def _(pe):
            def prologue():
                pe.wait_ge(load, 16 * 5)
                pe.wait_ge(ready, 2)
                nc.tensor.matmul(T[:, P:P + D], sm[:, 0:P], sm[:, 256:320], start=True, stop=True)
                nc.tensor.matmul(T[:, P + D:2 * P], sm[:, P:2 * P], sm[:, 320:384], start=True, stop=True)
                nc.tensor.matmul(T[:, 2 * P:2 * P + D], smc[:, :], sm[:, 384:448], start=True,
                                 stop=True).then_inc(folded, 1)
                pe.wait_ge(ready, 3)

            def scores(b, par, s):
                n = NS * b + s
                i, parts = CHUNKS[s]
                if due(n - 1):
                    pe.wait_ge(p_ready, n - 1)
                if s == 0:
                    for d in dup:
                        pe.wait_ge(d, 128 * (b + 1))
                    pe.wait_ge(mrow_in, 16 * (4 * b + 2))
                if s == LAST[1] + 1:
                    pe.wait_ge(mrow_in, 16 * (4 * b + 3))
                if s == LAST[2] + 1:
                    pe.wait_ge(mrow_in, 16 * (4 * b + 4))
                for kt, q0, w, col, mask in parts:
                    dst = S[s % 2][:, col:col + w]
                    qs = slice(QB * i + q0, QB * i + q0 + w)
                    ks = slice(P * kt, P * kt + P)
                    nc.tensor.matmul(dst, K1[par][:, ks], Q1[par][:, qs], start=True, stop=False)
                    ins = nc.tensor.matmul(dst, K2[par][:, ks], Q2[par][:, qs], start=False, stop=not mask)
                    if mask == "edge":
                        ins = nc.tensor.matmul(dst[:, 0:P], identb, edge, start=False, stop=True)
                    if mask == "full+edge":
                        ins = nc.tensor.matmul(dst, identb, full_edge, start=False, stop=True)
                ins.then_inc(s_full, 1)

            def values(b, par, s):
                i, parts = CHUNKS[s]
                first = s == 0 or CHUNKS[s - 1][0] != i
                pe.wait_ge(ph_ready, NS * b + s + 1)
                if s == 0:
                    pe.wait_ge(ones_in, b + 1)
                if first:
                    if due(4 * b + i):
                        pe.wait_ge(y_free, 4 * b + i)
                for low in range(2):
                    if low:
                        pe.wait_ge(pl_dve, NS * b + s + 1)
                        pe.wait_ge(pl_pool, by_pool(b, s))
                    for n, (kt, q0, w, col, _) in enumerate(parts):
                        last = s in LAST and n == len(parts) - 1 and low == 1
                        ins = nc.tensor.matmul(Y[:, q0:q0 + w], Xs[par][:, kt, :],
                                               (prob_l if low else prob_h)[s % PBUF][:, col:col + w],
                                               start=first and n == 0 and low == 0, stop=last)
                ins.then_inc(p_used, 1)

            def turn(k, c, nb, q):
                at = t_at(k, c, nb)
                if due(at):
                    pe.wait_ge(t_free, at)
                for j in range(TPB):
                    t = TPB * c + j
                    dst = T[:, P * j:P * j + P]
                    if k == "xT":
                        if j == 0 and c == 0:
                            pe.wait_ge(ln_l[0], nb + 1)
                        ins = nc.tensor.transpose(dst, Xs[q][:, t, :].bitcast(F32), ident)
                    if k == "proj":
                        if j == 0:
                            pe.wait_ge(t_free, t_at("xT", c, nb) + 1)
                        ins = nc.tensor.matmul(dst, XT[:, P * j:P * j + P], wqk[:, :], start=True, stop=True)
                    if k == "kT":
                        if j == 0:
                            pe.wait_ge(split, 4 * nb + c + 1)
                        ins = nc.tensor.transpose(dst, QKs[:, j, 2 * D:4 * D].bitcast(F32), ident)
                    if k == "qT":
                        ins = nc.tensor.transpose(dst, QKs[:, j, 0:2 * D].bitcast(F32), ident)
                if k == "mT":
                    pe.wait_ge(nm_ready, 4 * nb + c + 1)
                    ins = nc.tensor.transpose(T[0:TPB, 0:P], nm[c % 2][:, :], ident)
                ins.then_inc(t_full, 1)

            def piece(n, nb, q):
                t, g = PIECES[n]
                c = t // TPB
                if t % TPB == 0 and g == 0:
                    pe.wait_ge(dup[c % 2], 64 * (2 * nb + c // 2 + 1))
                bank, since = max_bank(n, nb)
                if due(NM * nb + n - since + 1):
                    pe.wait_ge(m_free, NM * nb + n - since + 1)
                w = min(QB, P * (t + 1) - QB * g)
                last = g == c
                nc_w = max(w, 2 * P)
                ins = nc.tensor.matmul(bank[:, 0:nc_w], Q1[q][:, P * t:P * t + P],
                                       K1[q][:, QB * g:QB * g + nc_w], start=True, stop=not last)
                if last:
                    ins = nc.tensor.matmul(bank[:, w - P:w], identb, edge_q, start=False, stop=True)
                ins.then_inc(m_full, 1)

            def mlp(k, c, b):
                if due(f_at(k, c, b)) and not (is_last(b) and k != "attn"):
                    pe.wait_ge(f_free, f_at(k, c, b))
                bank, x2t, h, w = mlp_buffers(c, b)
                if k == "attn":
                    pe.wait_ge(y_free, 4 * b + c + 1 if c < NF0 else 4 * b + c - 3)
                    for j in range(TPB):
                        ins = nc.tensor.matmul(F[:, P * j:P * j + P], YS[:, P * j:P * j + P], wv[:, :],
                                               start=True, stop=True)
                if k == "x2T":
                    if c == 0:
                        pe.wait_ge(ln_l[1], b)
                    for j in range(TPB):
                        ins = nc.tensor.transpose(bank[:, P * j:P * j + P], X2s[:, TPB * c + j, :].bitcast(F32), ident)
                if k == "in":
                    pe.wait_ge(f_free, f_at("x2T", c, b) + 1)
                    nc.tensor.matmul(bank, wi_h[:, :], x2t, start=True, stop=False)
                    ins = nc.tensor.matmul(bank, wi_l[:, :], x2t, start=False, stop=True)
                if k in ("mlp0", "mlp1"):
                    layer = int(k[3])
                    pe.wait_ge(f_free, f_at("in" if layer == 0 else "mlp0", c, b) + 1)
                    if layer == 0:
                        pe.wait_ge(w_in[c % 2], 64 * BATCH if is_last(b) else 32 * (2 * (b - 1) + c // 2 + 1))
                    for r in range(2):
                        cols = slice(ROUTED * r, ROUTED * r + ROUTED)
                        ins = nc.tensor.matmul(bank[:, cols], w[:, r, HID * layer:HID * layer + HID],
                                               h[:, cols], start=True, stop=True)
                if k == "out":
                    pe.wait_ge(f_free, f_at("mlp1", c, b) + 1)
                    for j in range(TPB):
                        ins = nc.tensor.matmul(bank[:, P * j:P * j + WOW], h[:, P * j:P * j + P],
                                               wo_sb[:, :], start=True, stop=True)
                ins.then_inc(f_full, 1)

            def step(b, par, s):
                attends, before, prepares, _ = on(b)
                if s == 0 and isinstance(b, int) and b == 0:
                    pe.wait_ge(ready, 4)
                    pe.wait_ge(m_free, sum(MAX_FIRST.values()))
                if attends:
                    scores(b, par, s)
                todo = [(n, nb, par if left else 1 - par) for n, nb, left in pieces(b, s)]
                half = (len(todo) + 1) // 2
                for point in range(2):
                    if point == 1:
                        lb, lpar, ls = lagging(b, par, s, LAG)
                        if exists(lb):
                            values(lb, lpar, ls)
                    now = todo[half:] if point else todo[:half]
                    if now:
                        piece(*now.pop(0))
                    for (ev, pt, k, c) in t_events(b):
                        if pt == point and ev == s and prepares:
                            turn(k, c, b + 1, 1 - par)
                        if pt == point and ev - NS == s and attends:
                            turn(k, c, b, par)
                    for one in now:
                        piece(*one)
                    for (ev, pt, k, c) in f_events(b):
                        if pt == point and ev == s and (attends if k == "attn" and c < NF0 else before):
                            mlp(k, c, b)
            run(pe, prologue, step)

        @block.vector
        def _(dve):
            def prologue():
                v = nc.vector
                dve.wait_ge(ids_in, 16)
                v.tensor_copy(ids_f[:, 0, :], ids_i[:, :])
                v.memset(rows_all[:, P:P + TILES].bitcast(F32), 0.0)
                v.drain()
                v.tensor_scalar(ids_f[:, 1, :], ids_f[:, 0, :], 0.0, float(VOCAB), ALU.is_lt, ALU.mult)
                v.drain()
                v.tensor_tensor(ids_f[:, 0, :], ids_f[:, 0, :], ids_f[:, 1, :], ALU.add)
                v.drain()
                v.tensor_scalar(ids_f[:, 0, :], ids_f[:, 0, :], 0.0, float(VOCAB - 1), ALU.max, ALU.min)
                v.drain()
                v.tensor_scalar(rows_all[:, 0:P], ids_f[:, 0, :], float(HIDDEN // D), float(SLICE), ALU.mult, ALU.add)
                v.drain()
                v.tensor_copy(rows_now[:, :], rows_all[:, 0:TILES]).then_inc(rows_ready, 1)
                v.memset(wo_sb[:, :], 0.0).then_inc(ready, 1)
                v.memset(wv[:, :], 0.0)
                dve.wait_ge(load, 16 * 5)
                v.tensor_scalar(smc[:, 0:D], sm[:, P:P + D], sm[:, P + D - 1:P + D], None, ALU.subtract)
                v.drain()
                v.tensor_copy(smc[:, D:P], smc[:, 0:D]).then_inc(ready, 1)
                v.tensor_copy(conb[:, 0:P], ident)
                v.tensor_copy(conb[:, P:4 * P], con)
                v.tensor_copy(wi_h[:, :], wi_sb[:, :])
                v.drain()
                v.tensor_tensor(wi_l[:, :], wi_sb[:, :], wi_h[:, :].bitcast(F32), ALU.subtract)
                dve.wait_ge(folded, 1)
                v.tensor_scalar(wqk[:, 0:D], T[:, P:P + D], D ** -0.5, None, ALU.mult)
                v.tensor_copy(wqk[:, D:P], T[:, P + D:2 * P])
                v.tensor_copy(wv[:, 0:D], T[:, 2 * P:2 * P + D])
                v.tensor_copy(wv[:, D:D + 1], ident[:, D - 1:D]).then_inc(ready, 1)
                for n in range(2):
                    v.memset(O[n][:, :, :], 0.0).then_inc(out_dma[n], 16)
                for q in (K2[0], Q2[0], K2[1], Q2[1]):
                    v.memset(q[D:P, :].bitcast(F32), 0.0)
                v.drain()
                for n in range(2):
                    v.memset(K2[n][D:D + 1, :].bitcast(F32), 1.0)

            def mlp_weights():
                v = nc.vector
                dve.wait_ge(load2, 16 * 8)
                for layer in range(N_LAYERS):
                    w = experts[:, N_EXPERTS, HID * layer:HID * layer + HID]
                    v.tensor_tensor(w, w, ident, ALU.add)
                v.drain()
                v.tensor_tensor(experts[:, 0:N_EXPERTS, :], experts[:, 0:N_EXPERTS, :],
                                experts[:, N_EXPERTS:N_EXPERTS + 1, :].broadcast_to([P, N_EXPERTS, EW]), ALU.add)
                v.tensor_copy(route_f[:, 0], route_i[:, :])
                v.drain()
                v.tensor_scalar(route_f[:, 1], route_f[:, 0], 0.0, None, ALU.is_ge)
                v.tensor_scalar(route_f[:, 2], route_f[:, 0], float(N_EXPERTS - 1), None, ALU.is_le)
                v.drain()
                v.tensor_tensor(route_f[:, 1], route_f[:, 1], route_f[:, 2], ALU.mult)
                v.tensor_scalar(route_f[:, 0], route_f[:, 0], -1.0, float(N_EXPERTS), ALU.max, ALU.min)
                v.drain()
                v.tensor_scalar(route_f[:, 0], route_f[:, 0], float(-N_EXPERTS), None, ALU.add)
                v.drain()
                v.tensor_tensor(route_f[:, 0], route_f[:, 0], route_f[:, 1], ALU.mult)
                v.drain()
                v.tensor_scalar(route_e[:, :], route_f[:, 0], float(N_EXPERTS), None, ALU.add).then_inc(ready, 1)

            def sums(n, which, src):
                nc.vector.tensor_reduce(stat[n][:, 2 * which, :], src, AX.X, ALU.add).then_inc(
                    (ln_sum if which == 0 else ln_var)[n], 1)

            def low_part(n, xs):
                nc.vector.tensor_tensor(xs[:, :, D:P], xn[n][:, :, :], xs[:, :, 0:D].bitcast(F32),
                                        ALU.subtract).then_inc(ln_l[n], 1)

            def reduce_piece(n, nb):
                t, g = PIECES[n]
                c = t // TPB
                w = min(QB, P * (t + 1) - QB * g)
                dve.wait_ge(m_full, NM * nb + n + 1)
                nc.vector.tensor_reduce(pm[c % 2][:, t % TPB, g:g + 1], max_bank(n, nb)[0][:, 0:w], AX.X, ALU.max).then_inc(m_free, 1)
                if t % TPB == TPB - 1 and g == c:
                    nc.vector.drain()
                    nc.vector.tensor_reduce(nm[c % 2][:, :], pm[c % 2][:, :, 0:c + 1], AX.X, ALU.max).then_inc(nm_ready, 1)
                    nc.vector.drain()

            def step(b, par, s):
                v = nc.vector
                attends, before, prepares, looks = on(b)
                if s == 1 and isinstance(b, int) and b == -1:
                    mlp_weights()
                if s == 0 and looks and not (isinstance(b, int) and b == -2):
                    if due(256 * (b + 2)):
                        dve.wait_ge(gathered, 256 * (b + 2))
                    v.tensor_copy(rows_now[:, :], rows_all[:, bass.ds(TILES * (b + 2), TILES)]).then_inc(rows_ready, 1)
                if s == 17 and looks:
                    dve.wait_ge(gathered, 256 * (b + 3))
                    sums(0, 0, G[par][:, :, :])
                if s == 19 and looks:
                    dve.wait_ge(ln_sq[0], b + 3)
                    sums(0, 1, xn[1][:, :, :])
                todo = pieces(b, s)
                half = (len(todo) + 1) // 2
                for point in range(2):
                    for n, nb, _ in (todo[half:] if point else todo[:half]):
                        reduce_piece(n, nb)
                    lb, _, ls = lagging(b, par, s, 1)
                    if point == 0 and s == 3 and prepares:
                        dve.wait_ge(ln_h[0], b + 2)
                        low_part(0, Xs[1 - par])
                    if point == 0 and exists(lb):
                        _, w = cut(ls)
                        dve.wait_ge(p_ready, NS * lb + ls + 1)
                        v.tensor_tensor(prob_l[ls % PBUF][:, 0:w], prob[ls % 2][:, 0:w],
                                        prob_h[ls % PBUF][:, 0:w].bitcast(F32),
                                        ALU.subtract).then_inc(pl_dve, 1)
                    for (ev, pt, k, c) in t_events(b):
                        if point == 0 or not prepares:
                            continue
                        if k == "proj" and ev + 1 == s:
                            dve.wait_ge(roped, 4 * (b + 1) + c + 1)
                            if c > 0:
                                dve.wait_ge(t_full, t_at("qT", c - 1, b + 1) + 1)
                            v.tensor_copy(QKs[:, :, D:3 * D], QK[:, :, :])
                            v.drain()
                            low = QKs[:, :, :].rearrange("p t (f d) -> p t f d", f=4)[:, :, 0:4:3, :]
                            high = QKs[:, :, D:3 * D].rearrange("p t (a d) -> p t a d", a=2)
                            v.tensor_tensor(low, QK[:, :, :].rearrange("p t (a d) -> p t a d", a=2),
                                            high.bitcast(F32), ALU.subtract).then_inc(split, 1)
                        if k == "qT" and c == 3 and ev == s:
                            dve.wait_ge(t_full, t_at("xT", 3, b + 1) + 1)
                            v.memset(Xs[1 - par][:, :, D - 1:D].bitcast(F32), 1.0)
                            v.memset(Xs[1 - par][:, :, P - 1:P].bitcast(F32), 0.0).then_inc(ones_in, 1)
                    for (ev, pt, k, c) in f_events(b):
                        if pt != point or ev != s:
                            continue
                        if k == "attn" and (attends if c < NF0 else before):
                            hb, q = (b, par) if c < NF0 else (b - 1, 1 - par)
                            tiles = slice(TPB * c, TPB * c + TPB)
                            dve.wait_ge(f_full, f_at(k, c, b) + 1)
                            dve.wait_ge(hres_in, 16 * (hb + 1))
                            f = F[:, :].rearrange("p (t n) -> p t n", n=P)
                            v.reciprocal(rec[:, :].unsqueeze(2), f[:, :, D:D + 1])
                            v.drain()
                            v.tensor_tensor(att[:, :, :], f[:, :, 0:D], rec[:, :].unsqueeze(2).broadcast_to([P, TPB, D]),
                                            ALU.mult).then_inc(f_free, 1)
                            v.drain()
                            v.tensor_tensor(H1[q][:, tiles, :], att[:, :, :], H1[q][:, tiles, :],
                                            ALU.add).then_inc(h1_done, 1)
                        if k == "out" and before:
                            dve.wait_ge(f_full, f_at(k, c, b) + 1)
                            dve.wait_ge(h1b_ready, b)
                            dve.wait_ge(out_dma[c % 2], 16 * (2 * (b - 1) + c // 2 + 1))
                            f = mlp_buffers(c, b)[0].rearrange("p (t n) -> p t n", n=P)
                            v.tensor_tensor(O[c % 2][:, :, :], f[:, :, 0:D], H1b[:, TPB * c:TPB * c + TPB, :],
                                            ALU.add).then_inc(o_free if is_last(b) else f_free, 1)

                if s == 8 and before:
                    dve.wait_ge(ln_h[1], b)
                    low_part(1, X2s)
                if s == 2 and before:
                    v.drain()
                    sums(1, 0, H1[1 - par][:, :, :])
                if s == 4 and before:
                    dve.wait_ge(ln_sq[1], b)
                    sums(1, 1, xn[0][:, :, :])
            run(dve, prologue, step)


_DTYPES = {"float32": F32, "int32": I32}


def shape_constants():
    k, q = np.arange(P)[:, None], np.arange(P)[None, :]
    edge = np.where(k > q, np.float32(NEG), np.float32(0))
    full = np.full((P, P), NEG, np.float32)
    consts = np.concatenate([np.eye(P, dtype=np.float32), full, edge, edge.T], axis=1)
    half = ROPE // 2
    theta = np.float32(1.0) / np.float32(10000.0) ** (np.arange(half, dtype=np.float32) / np.float32(half))
    angle = (np.arange(SEQ, dtype=np.float32)[:, None] * theta[None, :]).astype(np.float32)
    sin, cos = np.sin(angle), np.cos(angle)
    cos2 = np.repeat(cos, 2, axis=1)
    sin2 = np.stack([-sin, sin], axis=-1).reshape(SEQ, ROPE)
    tabs = np.stack([cos2, sin2]).reshape(2, TILES, P, 1, ROPE)
    tabs = np.broadcast_to(tabs, (2, TILES, P, 2, ROPE)).transpose(2, 0, 1, 3, 4)
    return np.ascontiguousarray(consts, np.float32), np.ascontiguousarray(tabs, np.float32)


def kernel(**inputs):
    import concourse.bacc as _bacc
    from concourse.bass_utils import run_bass_kernel_spmd as _run

    a = {k: np.asarray(v) for k, v in inputs.items()}
    at, ff = "L0_attn_", "L0_ffn_"
    consts, rope = shape_constants()
    wq, wkv = a[at + "Wq_comp"].T, a[at + "Wkv_comp"].T
    small = np.concatenate([wq, wq, wkv, wkv, a[at + "Wqc"], a[at + "Wqr"], a[at + "Wkc"], a[at + "Wkr"],
                            a[at + "Wv"]], axis=1)
    wit = a[ff + "Wi"].T
    arrays = {
        "ids": a["x"].reshape(P, P).T,
        "table": a["L0_tok_ple_table"],
        "consts": consts,
        "rope": rope,
        "small": small,
        "wi": np.concatenate([wit, wit], axis=0),
        "wo": a[ff + "Wo"].T,
        "wr": a[ff + "Wr"].transpose(3, 1, 0, 2).reshape(P, N_EXPERTS, N_LAYERS * HID),
        "ws": a[ff + "Ws"][:, 0].transpose(2, 0, 1).reshape(P, N_LAYERS * HID),
        "brt": a[ff + "br"].transpose(2, 1, 0),
        "bst": a[ff + "bs"][:, 0].T,
        "bi": a[ff + "bi"].reshape(P, 1),
        "bo": np.broadcast_to(a[ff + "bo"], (P, D)),
        "route": a[ff + "route_id"].reshape(1, 64),
    }
    nc = _bacc.Bacc("TRN2", target_bir_lowering=False, num_devices=1)
    feeds, args = {}, []
    for name, v in arrays.items():
        v = np.ascontiguousarray(v)
        feeds[f"in_{name}"] = v
        args.append(nc.dram_tensor(f"in_{name}", v.shape, _DTYPES[v.dtype.name], kind="ExternalInput").ap())
    args.append(nc.dram_tensor("out_0", (BATCH, SEQ, D), F32, kind="ExternalOutput").ap())
    tower_kernel(nc, *args)
    r = _run(nc, [feeds], core_ids=[0])
    return r.results[0]["out_0"]
```

```python
from contextlib import ExitStack

import concourse.bass as bass
import numpy as np
from concourse import mybir
from concourse.alu_op_type import AluOpType as ALU

ACT = mybir.ActivationFunctionType
AX = mybir.AxisListType
F32 = mybir.dt.float32
F32R = mybir.dt.float32r
BF16 = mybir.dt.bfloat16
I32 = mybir.dt.int32

P = 128
D = 64
BATCH, SEQ = 8, 2048
VOCAB, HIDDEN = 32000, 512
SLICE = 3
ROPE = 16
HID, N_LAYERS, N_EXPERTS = 128, 2, 16
ROUTED = BATCH * SEQ // 64
EPS = 1e-5

TILES = SEQ // P
QB = 512
BLOCKS = SEQ // QB
TPB = QB // P
EW = N_LAYERS * HID + N_LAYERS
WOW = 96
NEG = -1e30


def attention_chunks():
    chunks = []
    for i in range(BLOCKS):
        for kt in range(0, TPB * i, 2):
            chunks.append((i, [(kt, 0, QB, 0, ""), (kt + 1, 0, QB, QB, "")]))
        k = TPB * i
        chunks.append((i, [(k, 0, 512, 0, "edge"), (k + 1, 128, 384, 512, "edge")]))
        chunks.append((i, [(k + 2, 256, 256, 0, "edge"), (k + 3, 256, 256, 256, "full+edge")]))
    return chunks


CHUNKS = attention_chunks()
NS = len(CHUNKS)
LAST = [max(n for n, ch in enumerate(CHUNKS) if ch[0] == i) for i in range(BLOCKS)]
PBUF = 3
DVE_ALONE = (6, 7)
LAG = 2


def max_pieces():
    return [(t, g) for t in range(TILES) for g in range(t // TPB + 1)]


PIECES = max_pieces()
NM = len(PIECES)

MT_AT = (12.5, 16, NS + 2, NS + 9.5)
T_EVENTS = sorted(
    [(3 * c + 4, 0, "xT", c) for c in range(BLOCKS)]
    + [(3 * c + 5, 0, "proj", c) for c in range(BLOCKS)]
    + [(3 * c + 7, 1, "kT", c) for c in range(BLOCKS)]
    + [(3 * c + 8, 1, "qT", c) for c in range(BLOCKS)]
    + [(int(s), int(s % 1 > 0), "mT", c) for c, s in enumerate(MT_AT)]
)
NT = len(T_EVENTS)
T_FIRST = sorted([e for e in T_EVENTS if e[2] != "mT"] + [(14, 1, "mT", 0), (17, 1, "mT", 1)])
T_ORDER = [(k, c) for _, _, _, k, c in sorted((s % NS, pt, s >= NS, k, c) for s, pt, k, c in T_EVENTS)]
T_TAIL = [(k, c) for s, _, k, c in T_EVENTS if s >= NS]
MAX_AT = {11: 3, 12: 1,
          13: 2, 14: 3, 15: 3,
          16: 2, 17: 3, 18: 2, 19: 3, NS: 1, NS + 1: 1,
          NS + 2: 2, NS + 3: 1, NS + 4: 2, NS + 5: 2, NS + 6: 2, NS + 7: 3, NS + 8: 3, NS + 9: 1}
assert sum(MAX_AT.values()) == NM
MAX_FIRST = {12: 2, 13: 2, 15: 4, 16: 4, 17: 3, 18: 3, 19: 4}
assert sum(MAX_FIRST.values()) == sum(n for s, n in MAX_AT.items() if s < NS)
GATHER_FIRST = [0, 1, 0, 0, 0, 1, 2, 3, 1, 1, 2, 1, 1, 1, 2, 0, 0, 0, 0, 0]
assert len(GATHER_FIRST) == NS and sum(GATHER_FIRST) == TILES
F_EVENTS = sorted(
    [(h // 2, h % 2, "attn", i) for i, h in enumerate((8, 16, 2, 4))]
    + [(min(h + 2 * j, 2 * NS - 1) // 2, min(h + 2 * j, 2 * NS - 1) % 2, k, c) for c, h in enumerate((19, 22, 29, 32))
       for j, k in enumerate(("x2T", "in", "mlp0", "mlp1", "out")) if (j, c) != (0, 0)]
    + [(10, 0, "x2T", 0)])
NF = len(F_EVENTS)
USES = ("x2T", "in", "mlp0", "mlp1", "out")
F_LAST = [(1, 0, "attn", 2), (2, 0, "attn", 3)] + [(9 + 2 * j, 0, k, c) for j, k in enumerate(USES)
                                                  for c in range(BLOCKS)]
NF0 = 2
F_ORD0 = {("attn", i): i for i in range(NF0)}


def tower_kernel(nc, ids, table, consts, rope, small, wi, wo, wr, ws, brt, bst, bi, bo, route, out):
    table_rows = table.rearrange("v (s d) -> (v s) d", d=D)
    out_v = out.rearrange("b (t p) d -> b p t d", p=P)

    with ExitStack() as ctx:
        def sb(name, shape, dt=F32):
            return ctx.enter_context(nc.sbuf_tensor(name, shape, dt))

        def bank(name, n=1):
            return ctx.enter_context(nc.psum_tensor(name, [P, 512 * n], F32))

        def sem(name):
            return ctx.enter_context(nc.semaphore(name))

        ident = sb("ident", [P, P])[:, :]
        conb = sb("conb", [P, 4 * P], BF16)
        identb, full_edge, edge, edge_q = conb[:, 0:P], conb[:, P:3 * P], conb[:, 2 * P:3 * P], conb[:, 3 * P:4 * P]
        rope_sb = sb("rope_sb", [P, 2, TILES, 2, ROPE])
        wqk = sb("wqk", [P, P])
        wv = sb("wv", [P, WOW])
        wi_sb = sb("wi_sb", [P, HID])
        wi_h = sb("wi_h", [P, HID], F32R)
        wi_l = sb("wi_l", [P, HID], F32R)
        wo_sb = sb("wo_sb", [P, WOW])
        experts = sb("experts", [P, N_EXPERTS + 1, EW])
        bi_sb = sb("bi_sb", [P, 1])
        bo_sb = sb("bo_sb", [P, D])
        route_i = sb("route_i", [1, 64], I32)
        route_f = sb("route_f", [1, 3, 64])
        route_e = sb("route_e", [1, 64], I32)
        rows_all = sb("rows_all", [P, P + TILES], I32)
        rows_now = sb("rows_now", [P, TILES], I32)
        gate = sb("gate", [P, 1])
        lnc = sb("lnc", [P, 3])
        G = [sb(f"G{n}", [P, TILES, D]) for n in range(2)]
        xn = [sb(f"xn{n}", [P, TILES, D]) for n in range(2)]
        stat = [sb(f"stat{n}", [P, 6, TILES]) for n in range(2)]
        Xs = [sb(f"Xs{n}", [P, TILES, P], F32R) for n in range(2)]
        XT = sb("XT", [P, QB])
        QK = sb("QK", [P, TPB, P])
        rt = sb("rt", [P, 2, TPB, 2, ROPE])
        QKs = sb("QKs", [P, TPB, 4 * D], F32R)
        QT = sb("QT", [P, QB], F32R)
        K1 = [sb(f"K1{n}", [P, SEQ], F32R) for n in range(2)]
        K2 = [sb(f"K2{n}", [P, SEQ], F32R) for n in range(2)]
        Q1 = [sb(f"Q1{n}", [P, SEQ], F32R) for n in range(2)]
        Q2 = [sb(f"Q2{n}", [P, SEQ], F32R) for n in range(2)]
        pm = [sb(f"pm{n}", [P, TPB, BLOCKS]) for n in range(2)]
        nm = [sb(f"nm{n}", [P, TPB]) for n in range(2)]
        mrow = sb("mrow", [TPB, P], F32R)
        prob_h = [sb(f"prob_h{n}", [P, 1024], F32R) for n in range(PBUF)]
        prob_l = [sb(f"prob_l{n}", [P, 1024], F32R) for n in range(PBUF)]
        prob = [sb(f"prob{n}", [P, 1024]) for n in range(2)]
        con = prob[0][:, 0:3 * P]
        sm = prob[1][0:D, 0:448]
        smc = prob[1][0:D, QB:QB + P]
        ids_i = prob[0][:, 3 * P:4 * P].bitcast(I32)
        ids_f = prob[0][:, 4 * P:6 * P].rearrange("p (n t) -> p n t", n=2)
        YS = sb("YS", [P, QB])
        rec = sb("rec", [P, TPB])
        att = sb("att", [P, TPB, D])
        H1 = [sb(f"H1{n}", [P, TILES, D]) for n in range(2)]
        H1b = sb("H1b", [P, TILES, D])
        X2s = sb("X2s", [P, TILES, P], F32R)
        X2T = sb("X2T", [P, QB], F32R)
        hid = [sb(f"hid{n}", [P, QB]) for n in range(2)]
        wexp = [sb(f"wexp{n}", [P, 2, EW]) for n in range(2)]
        O = [sb(f"O{n}", [P, TPB, D]) for n in range(2)]

        S = [bank(f"S{n}", 2) for n in range(2)]
        Y = bank("Y")
        M = bank("M")
        T = bank("T")
        F = bank("F")

        ids_in = sem("ids_in")
        load = sem("load")
        load2 = sem("load2")
        ready = sem("ready")
        folded = sem("folded")
        rows_ready = sem("rows_ready")
        gathered0 = sem("gathered0")
        gathered = sem("gathered")
        half_xc = sem("half_xc")
        half_sq = sem("half_sq")
        half_var = sem("half_var")
        half_rstd = sem("half_rstd")
        half_x = sem("half_x")
        half_h = sem("half_h")
        half_l = sem("half_l")
        hres_in = sem("hres_in")
        ln_sum = [sem(f"ln_sum{n}") for n in range(2)]
        ln_xc = [sem(f"ln_xc{n}") for n in range(2)]
        ln_var = [sem(f"ln_var{n}") for n in range(2)]
        ln_sq = [sem(f"ln_sq{n}") for n in range(2)]
        ln_x = [sem(f"ln_x{n}") for n in range(2)]
        ln_h = [sem(f"ln_h{n}") for n in range(2)]
        ln_l = [sem(f"ln_l{n}") for n in range(2)]
        ones_in = sem("ones_in")
        turned = sem("turned")
        roped = sem("roped")
        split = sem("split")
        dup = [sem(f"dup{n}") for n in range(2)]
        mrow_in = sem("mrow_in")
        nm_ready = sem("nm_ready")
        s_full = sem("s_full")
        ph_ready, p_ready = sem("ph_ready"), sem("p_ready")
        pl_dve, pl_pool = sem("pl_dve"), sem("pl_pool")
        p_used = sem("p_used")
        y_free = sem("y_free")
        m_full, m_free = sem("m_full"), sem("m_free")
        t_full, t_free = sem("t_full"), sem("t_free")
        f_full, f_free = sem("f_full"), sem("f_free")
        o_free = sem("o_free")
        h1_done = sem("h1_done")
        h1b_ready = sem("h1b_ready")
        w_in = [sem(f"w_in{n}") for n in range(2)]
        out_dma = [sem(f"out_dma{n}") for n in range(2)]

        def due(n):
            return not isinstance(n, int) or n > 0

        def t_at(k, c, b):
            tail = (k, c) in T_TAIL
            if isinstance(b, int) and b == 0 and not tail:
                return [(k_, c_) for _, _, k_, c_ in T_FIRST].index((k, c))
            n = T_ORDER.index((k, c))
            if isinstance(b, int) and b == BATCH - 1 and tail:
                n = T_TAIL.index((k, c))
            return NT * (b + tail) - len(T_TAIL) + n

        def t_events(it):
            return T_FIRST if isinstance(it, int) and it == -1 else T_EVENTS

        def t_bank(k, c, nb):
            if isinstance(nb, int) and nb == 0 and (k, c) not in T_TAIL and t_at(k, c, 0) % 2:
                return F
            return T

        def is_last(it):
            return isinstance(it, int) and it == BATCH

        def f_events(it):
            return F_LAST if is_last(it) else F_EVENTS

        def mlp_buffers(c, it):
            if not is_last(it):
                return F[:, :], X2T[:, :], hid[c % 2][:, :], wexp[c % 2][:, :, :]
            cols = slice(QB * (c % 2), QB * (c % 2) + QB)
            w = wexp[c][:, :, :] if c < 2 else G[c - 2][:, :, :].rearrange("p t d -> p (t d)")[
                :, 0:2 * EW].rearrange("p (r n) -> p r n", r=2)
            return S[c // 2][:, cols], prob_h[c // 2][:, cols], prob[c // 2][:, cols], w

        def f_at(k, c, it):
            if isinstance(it, int) and it == 0:
                return F_ORD0[k, c]
            n = [(k_, c_) for _, _, k_, c_ in f_events(it)].index((k, c))
            return NF * it + (NF0 - NF) + n

        def piece_at(table, s):
            first = sum(n for x, n in table.items() if x < s)
            return list(range(first, first + table.get(s, 0)))

        def pieces(b, s):
            attends, _, prepares, _ = on(b)
            own = piece_at(MAX_FIRST if isinstance(b, int) and b == -1 else MAX_AT, s)
            return ([(n, b + 1, False) for n in own] if prepares else []) + (
                [(n, b, True) for n in piece_at(MAX_AT, NS + s)] if attends else [])

        def borrowed(b, s):
            todo = pieces(b, s)
            return todo[:(len(todo) + 1) // 2] if len(todo) > 1 else []

        in_m = [n for s in sorted(MAX_AT) for n in piece_at(MAX_AT, s)[(MAX_AT[s] + 1) // 2 if MAX_AT[s] > 1 else 0:]]
        first_banks = [M[:, :]] + [S[n][:, QB * m:QB * m + QB] for n in range(2) for m in range(2)]

        def max_bank(n, nb, s):
            if isinstance(nb, int) and nb == 0 and n < sum(MAX_FIRST.values()):
                return first_banks[n % 5]
            if n in in_m:
                return M[:, :]
            m = piece_at(MAX_AT, s if n in piece_at(MAX_AT, s) else s + NS).index(n)
            return S[(s + 1) % 2][:, QB * m:QB * m + QB]

        def lagging(b, par, s, lag):
            return (b, par, s - lag) if s >= lag else (b - 1, 1 - par, s - lag + NS)

        HALF = [slice(0, TILES // 2), slice(TILES // 2, TILES)]

        def is_it(b, n):
            return isinstance(b, int) and b == n

        def exists(b):
            return not isinstance(b, int) or 0 <= b < BATCH

        def cut(s):
            _, parts = CHUNKS[s]
            width = parts[-1][3] + parts[-1][2]
            return width, width if s in DVE_ALONE else width // 2

        def by_pool(b, s):
            return (NS - len(DVE_ALONE)) * b + sum(1 for m in range(s + 1) if m not in DVE_ALONE)

        def iteration(step_of, b, par):
            for s in range(NS):
                step_of(b, par, s)

        def run(eng, prologue, step_of):
            prologue()
            for b in (-2, -1, 0):
                iteration(step_of, b, b % 2)
            with eng.Fori(0, 3) as j:
                iteration(step_of, j * 2 + 1, 1)
                iteration(step_of, j * 2 + 2, 0)
            for b in (7, 8):
                iteration(step_of, b, b % 2)

        def on(b):
            if not isinstance(b, int):
                return True, True, True, True
            return 0 <= b < BATCH, 0 < b <= BATCH, -1 <= b < BATCH - 1, b < BATCH - 2

        block = ctx.enter_context(nc.Block())

        @block.sync
        def _(sp):
            def prologue():
                sp.dma_start(ids_i, ids).then_inc(ids_in, 16)
                sp.dma_start(ident, consts[:, 0:P]).then_inc(load, 16)
                sp.dma_start(con, consts[:, P:4 * P]).then_inc(load, 16)
                sp.dma_start(sm, small).then_inc(load, 16)
                sp.dma_start(rope_sb[:, :, :, :, :], rope).then_inc(load, 16)
                sp.dma_start(wi_sb[:, :], wi).then_inc(load, 16)
                sp.dma_start(route_i[:, :], route).then_inc(load2, 16)
                sp.dma_start(bi_sb[:, :], bi).then_inc(load2, 16)
                sp.dma_start(bo_sb[:, :], bo).then_inc(load2, 16)
                sp.dma_start(experts[:, N_EXPERTS, 0:2 * HID], ws).then_inc(load2, 16)
                sp.dma_start(experts[:, N_EXPERTS, 2 * HID:EW], bst).then_inc(load2, 16)
                sp.dma_start(experts[:, 0:N_EXPERTS, 0:2 * HID], wr).then_inc(load2, 16)
                sp.dma_start(experts[:, 0:N_EXPERTS, 2 * HID:EW], brt).then_inc(load2, 16)
                sp.wait_ge(ready, 1)
                sp.dma_start(wo_sb[:, 0:D], wo).then_inc(load2, 16)

            def step(b, par, s):
                attends, before, prepares, _ = on(b)
                if s == NS - 1 and is_it(b, 0):
                    sp.wait_ge(ready, 4)
                if s == 13 and prepares:
                    if is_it(b, -1):
                        sp.wait_ge(gathered0, 16 * TILES // 2)
                    if isinstance(b, int):
                        sp.wait_ge(gathered, 256 * (b + 2) - 128)
                    if due(b):
                        sp.wait_ge(h1b_ready, b)
                    sp.dma_start(H1[1 - par][:, :, :], G[1 - par][:, :, :]).then_inc(hres_in, 16)
                for (ev, _, k, c) in t_events(b):
                    if ev == s and prepares:
                        nb = b + 1
                        cols = slice(QB * c, QB * c + QB)
                        if k == "kT":
                            sp.wait_ge(t_free, t_at("kT", c, nb) + 1)
                            sp.dma_start(K2[1 - par][0:D, cols].bitcast(F32),
                                         K1[1 - par][0:D, cols].bitcast(F32)).then_inc(dup[c % 2], 16)
                        if k == "qT":
                            sp.wait_ge(t_free, t_at("qT", c, nb) + 1)
                            for dst, src in ((Q1[1 - par][0:D, cols], QT[D:P, :]), (Q1[1 - par][D:P, cols], QT[D:P, :]),
                                             (Q2[1 - par][0:D, cols], QT[0:D, :])):
                                sp.dma_start(dst.bitcast(F32), src.bitcast(F32)).then_inc(dup[c % 2], 16)
                    tail = ev - NS == s and attends
                    if (ev == s and prepares or tail) and k == "mT":
                        nb, q = (b, par) if tail else (b + 1, 1 - par)
                        sp.wait_ge(t_free, t_at("mT", c, nb) + 1)
                        sp.dma_start(Q2[q][D:D + 1, QB * c:QB * c + QB].bitcast(F32),
                                     mrow[:, :].bitcast(F32)).then_inc(mrow_in, 16)
                for (ev, _, k, c) in f_events(b):
                    if k == "x2T" and s == ev - 2 and before:
                        if is_last(b):
                            if c == 2:
                                sp.wait_ge(hres_in, 16 * BATCH)
                        elif c >= 2:
                            sp.wait_ge(f_free, f_at("mlp1", c - 2, b) + 1)
                        for r in range(2):
                            e = sp.value_load(route_e[0:1, bass.ds(8 * (b - 1) + 2 * c + r, 1)],
                                              min_val=0, max_val=N_EXPERTS)
                            sp.dma_start(mlp_buffers(c, b)[3][:, r, :], experts[:, bass.ds(e, 1), :].rearrange(
                                "p a n -> p (a n)")).then_inc(w_in[c % 2], 16)
                    if k == "out" and s == ev and before:
                        if is_last(b):
                            sp.wait_ge(o_free, c + 1)
                        else:
                            sp.wait_ge(f_free, f_at("out", c, b) + 1)
                        sp.dma_start(out_v[bass.ds(b - 1, 1), :, TPB * c:TPB * c + TPB, :].rearrange(
                            "a p t d -> (a p) t d"), O[c % 2][:, :, :]).then_inc(out_dma[c % 2], 16)

            run(sp, prologue, step)
            for n in range(2):
                sp.wait_ge(out_dma[n], 16 * (2 * BATCH + 1))

        @block.gpsimd
        def _(pool):
            def prologue():
                nc.gpsimd.memset(gate[:, :], 0.0)
                for n, x in enumerate((1.0 / D, EPS, -0.5)):
                    nc.gpsimd.memset(lnc[:, n:n + 1], x)
                nc.gpsimd.drain()

            def centre(n, src):
                p, st = nc.gpsimd, stat[n]
                p.tensor_tensor(st[:, 1, :], st[:, 0, :], lnc[:, 0:1].broadcast_to([P, TILES]), ALU.mult)
                p.drain()
                p.tensor_tensor(xn[n][:, :, :], src, st[:, 1, :].unsqueeze(2).broadcast_to([P, TILES, D]),
                                ALU.subtract).then_inc(ln_xc[n], 1)

            def deviation(n, tiles):
                p, st = nc.gpsimd, stat[n]
                for row, op in ((2, ALU.mult), (3, ALU.add), (4, ALU.pow)):
                    if row > 2:
                        p.drain()
                    ins = p.tensor_tensor(st[:, row + 1, tiles], st[:, row, tiles],
                                          lnc[:, row - 2:row - 1].broadcast_to([P, tiles.stop - tiles.start]), op)
                return ins

            def normalise(n):
                p, st = nc.gpsimd, stat[n]
                deviation(n, slice(0, TILES))
                p.drain()
                p.tensor_tensor(xn[n][:, :, :], xn[n][:, :, :],
                                st[:, 5, :].unsqueeze(2).broadcast_to([P, TILES, D]), ALU.mult).then_inc(ln_x[n], 1)

            def step(b, par, s):
                attends, before, prepares, looks = on(b)
                lb, _, ls = lagging(b, par, s, 1)
                if exists(lb) and ls not in DVE_ALONE:
                    width, w = cut(ls)
                    pool.wait_ge(p_ready, NS * lb + ls + 1)
                    nc.gpsimd.tensor_tensor(prob_l[ls % PBUF][:, w:width], prob[ls % 2][:, w:width],
                                            prob_h[ls % PBUF][:, w:width].bitcast(F32),
                                            ALU.subtract).then_inc(pl_pool, 1)
                if s == 3 and before and not is_last(b):
                    pool.wait_ge(ln_sum[1], b)
                    centre(1, H1[1 - par][:, :, :])
                if s == 17 and looks and not is_it(b, -2):
                    pool.wait_ge(ln_sum[0], b + 2)
                    centre(0, G[par][:, :, :])
                if s == 19 and looks and not is_it(b, -2):
                    pool.wait_ge(ln_var[0], b + 2)
                    normalise(0)
                for (ev, _, k, c) in t_events(b):
                    if k == "proj" and ev == s and prepares:
                        nb = b + 1
                        pool.wait_ge(t_free, t_at("proj", c, nb) + 1)
                        r = QK[:, :, :].rearrange("p t (a d) -> p t a d", a=2)[:, :, :, D - ROPE:D]
                        cos, sin = (rope_sb[:, n, TPB * c:TPB * c + TPB] for n in range(2))
                        for half in range(2):
                            nc.gpsimd.tensor_tensor(rt[:, 1, :, :, half::2], r[:, :, :, 1 - half::2],
                                                    sin[:, :, :, half::2], ALU.mult)
                        nc.gpsimd.tensor_tensor(rt[:, 0], r, cos, ALU.mult).then_inc(turned, 1)
                        pool.wait_ge(turned, 4 * nb + c + 1)
                        nc.gpsimd.tensor_tensor(r, rt[:, 0], rt[:, 1], ALU.add).then_inc(roped, 1)
                if s == 6 and before and not is_last(b):
                    pool.wait_ge(ln_var[1], b)
                    normalise(1)
                if s == 1 and looks:
                    pool.wait_ge(rows_ready, b + 3)
                    if due(16 * (b + 1)):
                        pool.wait_ge(hres_in, 16 * (b + 1))
                    nc.gpsimd.tensor_tensor(gate[:, :], gate[:, :], gate[:, :], ALU.mult)
                done = sum(GATHER_FIRST[:s]) if is_it(b, -1) else max(s - 1, 0)
                for t in range(done, min(done + (GATHER_FIRST[s] if is_it(b, -1) else int(s > 0)), TILES) if looks else 0):
                    nc.gpsimd.indirect_dma_start(
                        out=G[par][:, t, :], out_offset=None, in_=table_rows,
                        in_offset=bass.IndirectOffsetOnAxis(ap=rows_now[:, t:t + 1], axis=0),
                    ).then_inc(gathered0 if is_it(b, -2) and t < TILES // 2 else gathered, 16)
                for it, at, h, n in ((-2, 13, 0, 0), (-1, 6, 1, 0), (7, 16, 0, 1), (8, 3, 1, 1)):
                    if not (is_it(b, it) and s == at):
                        continue
                    pool.wait_ge(half_var, 2 * n + h + 1)
                    deviation(n, HALF[h]).then_inc(half_rstd, 1)
                if s == 12 and before:
                    pool.wait_ge(h1_done, 4 * b)
                    if not isinstance(b, int) or b > 1:
                        pool.wait_ge(f_free, f_at("out", 3, b - 1) + 1)
                    nc.gpsimd.tensor_tensor(H1b[:, :, :], H1[1 - par][:, :, :],
                                            bo_sb[:, :].unsqueeze(1).broadcast_to([P, TILES, D]),
                                            ALU.add).then_inc(h1b_ready, 1)
            run(pool, prologue, step)

        @block.scalar
        def _(act):
            def prologue():
                act.wait_ge(load, 16 * 5)
                for n in range(2):
                    for q, col in ((K2[n], D), (Q2[n], 0)):
                        nc.scalar.activation(q[D:P, :], ident[D:P, col:col + 1].broadcast_to([P - D, SEQ]), ACT.Copy)

            def relu(dst, src, bias):
                return nc.scalar.activation(dst, src, ACT.Relu, bias=bias)

            def step(b, par, s):
                attends, before, prepares, looks = on(b)
                if attends:
                    n = NS * b + s
                    i, parts = CHUNKS[s]
                    width = parts[-1][3] + parts[-1][2]
                    act.wait_ge(s_full, n + 1)
                    same = [m for m in range(NS) if m % PBUF == s % PBUF]
                    used = NS * b + s - PBUF + 1 if s >= PBUF else NS * (b - 1) + same[-1] + 1
                    if due(used):
                        act.wait_ge(p_used, used)
                    nc.scalar.activation(prob_h[s % PBUF][:, 0:width], S[s % 2][:, 0:width],
                                         ACT.Exp).then_inc(ph_ready, 1)
                for point in range(2):
                    if point == 1 and attends:
                        if due(n - 1):
                            act.wait_ge(pl_dve, n - 1)
                            act.wait_ge(pl_pool, by_pool(b, s - 2) if s >= 2 else by_pool(b - 1, s - 2 + NS))
                        nc.scalar.activation(prob[s % 2][:, 0:width], S[s % 2][:, 0:width],
                                             ACT.Exp).then_inc(p_ready, 1)
                    lb, _, ls = lagging(b, par, s, LAG)
                    if point == 1 and exists(lb) and ls in LAST:
                        act.wait_ge(p_used, NS * lb + ls + 1)
                        nc.scalar.activation(YS[:, :], Y[:, :], ACT.Copy).then_inc(y_free, 1)
                    for (ev, pt, k, c) in t_events(b):
                        tail = ev - NS == s and attends
                        if pt != point or not (ev == s and prepares or tail):
                            continue
                        nb, q = (b, par) if tail else (b + 1, 1 - par)
                        act.wait_ge(t_full, t_at(k, c, nb) + 1)
                        cols = slice(QB * c, QB * c + QB)
                        if k == "xT":
                            ins = nc.scalar.activation(XT[:, :], t_bank(k, c, nb)[:, :], ACT.Copy)
                        if k == "proj":
                            ins = nc.scalar.activation(QK[:, :, :].rearrange("p t n -> p (t n)"), t_bank(k, c, nb)[:, :], ACT.Copy)
                        if k == "kT":
                            ins = nc.scalar.activation(K1[q][:, cols], t_bank(k, c, nb)[:, :], ACT.Copy)
                        if k == "qT":
                            if due(64 * (2 * nb + (c + 1) // 2)):
                                act.wait_ge(dup[(c + 1) % 2], 64 * (2 * nb + (c + 1) // 2))
                            ins = nc.scalar.activation(QT[:, :], t_bank(k, c, nb)[:, :], ACT.Copy)
                        if k == "mT":
                            if due(16 * (4 * nb + c)):
                                act.wait_ge(mrow_in, 16 * (4 * nb + c))
                            ins = nc.scalar.activation(mrow[:, :], t_bank(k, c, nb)[0:TPB, 0:P], ACT.Copy, scale=-1.0)
                        ins.then_inc(t_free, 1)
                    for (ev, pt, k, c) in f_events(b):
                        if pt != point or ev != s or not before or k in ("attn", "out"):
                            continue
                        act.wait_ge(f_full, f_at(k, c, b) + 1)
                        bank, x2t, h, w = mlp_buffers(c, b)
                        if k == "x2T":
                            ins = nc.scalar.activation(x2t, bank, ACT.Copy)
                        if k == "in":
                            ins = relu(h, bank, bi_sb[:, 0:1])
                        if k in ("mlp0", "mlp1"):
                            layer = int(k[3])
                            for r in range(2):
                                cols = slice(ROUTED * r, ROUTED * r + ROUTED)
                                ins = relu(h[:, cols], bank[:, cols],
                                           w[:, r, 2 * HID + layer:2 * HID + layer + 1])
                        ins.then_inc(f_free, 1)
                for it, at, h, n in ((-2, 5, 0, 0), (-1, 5, 1, 0), (7, 14, 0, 1), (8, 4, 1, 1)):
                    if is_it(b, it) and s == at:
                        act.wait_ge(half_xc, 2 * n + h + 1)
                        nc.scalar.activation(xn[1 - n][:, HALF[h], :], xn[n][:, HALF[h], :],
                                             ACT.Square).then_inc(half_sq, 1)
                for it, at, h, n in ((-2, 7, 0, 0), (-1, 7, 1, 0), (7, 18, 0, 1), (8, 8, 1, 1)):
                    if is_it(b, it) and s == at:
                        act.wait_ge(half_x, 2 * n + h + 1)
                        nc.scalar.activation((X2s if n else Xs[0])[:, HALF[h], 0:D], xn[n][:, HALF[h], :],
                                             ACT.Copy).then_inc(half_h, 1)
                if s == 2 and prepares and not is_it(b, -1):
                    act.wait_ge(ln_x[0], b + 1)
                    if due(NS * b):
                        act.wait_ge(p_used, NS * b)
                    nc.scalar.activation(Xs[1 - par][:, :, 0:D], xn[0][:, :, :], ACT.Copy).then_inc(ln_h[0], 1)
                if s == 4 and before and not is_last(b):
                    act.wait_ge(ln_xc[1], b)
                    act.wait_ge(ln_l[0], b + 1 if prepares else BATCH - 1)
                    nc.scalar.activation(xn[0][:, :, :], xn[1][:, :, :], ACT.Square).then_inc(ln_sq[1], 1)
                if s == 8 and before and not is_last(b):
                    act.wait_ge(ln_x[1], b)
                    nc.scalar.activation(X2s[:, :, 0:D], xn[1][:, :, :], ACT.Copy).then_inc(ln_h[1], 1)
                if s == 18 and looks and not is_it(b, -2):
                    act.wait_ge(ln_xc[0], b + 2)
                    if due(b):
                        act.wait_ge(ln_l[1], b)
                    nc.scalar.activation(xn[1][:, :, :], xn[0][:, :, :], ACT.Square).then_inc(ln_sq[0], 1)
            run(act, prologue, step)

        @block.tensor
        def _(pe):
            def prologue():
                pe.wait_ge(load, 16 * 5)
                pe.wait_ge(ready, 2)
                nc.tensor.matmul(T[:, P:P + D], sm[:, 0:P], sm[:, 256:320], start=True, stop=True)
                nc.tensor.matmul(T[:, P + D:2 * P], sm[:, P:2 * P], sm[:, 320:384], start=True, stop=True)
                nc.tensor.matmul(T[:, 2 * P:2 * P + D], smc[:, :], sm[:, 384:448], start=True,
                                 stop=True).then_inc(folded, 1)
                pe.wait_ge(ready, 3)

            def scores(b, par, s):
                n = NS * b + s
                i, parts = CHUNKS[s]
                if due(n - 1):
                    pe.wait_ge(p_ready, n - 1)
                pb, _, ps = lagging(b, par, s, 1)
                if exists(pb) and borrowed(pb, ps):
                    m, mb, _ = borrowed(pb, ps)[-1]
                    pe.wait_ge(m_free, NM * mb + m + 1)
                if s - 1 in LAST or s == 0:
                    pe.wait_ge(dup[i % 2], 64 * (2 * b + i // 2 + 1))
                    pe.wait_ge(mrow_in, 16 * (4 * b + i + 1))
                for kt, q0, w, col, mask in parts:
                    dst = S[s % 2][:, col:col + w]
                    qs = slice(QB * i + q0, QB * i + q0 + w)
                    ks = slice(P * kt, P * kt + P)
                    nc.tensor.matmul(dst, K1[par][:, ks], Q1[par][:, qs], start=True, stop=False)
                    ins = nc.tensor.matmul(dst, K2[par][:, ks], Q2[par][:, qs], start=False, stop=not mask)
                    if mask == "edge":
                        ins = nc.tensor.matmul(dst[:, 0:P], identb, edge, start=False, stop=True)
                    if mask == "full+edge":
                        ins = nc.tensor.matmul(dst, identb, full_edge, start=False, stop=True)
                ins.then_inc(s_full, 1)

            def values(b, par, s):
                i, parts = CHUNKS[s]
                first = s == 0 or CHUNKS[s - 1][0] != i
                pe.wait_ge(ph_ready, NS * b + s + 1)
                if s == 0:
                    pe.wait_ge(ones_in, b + 1)
                if first:
                    if due(4 * b + i):
                        pe.wait_ge(y_free, 4 * b + i)
                for low in range(2):
                    if low:
                        pe.wait_ge(pl_dve, NS * b + s + 1)
                        pe.wait_ge(pl_pool, by_pool(b, s))
                    for n, (kt, q0, w, col, _) in enumerate(parts):
                        last = s in LAST and n == len(parts) - 1 and low == 1
                        ins = nc.tensor.matmul(Y[:, q0:q0 + w], Xs[par][:, kt, :],
                                               (prob_l if low else prob_h)[s % PBUF][:, col:col + w],
                                               start=first and n == 0 and low == 0, stop=last)
                ins.then_inc(p_used, 1)

            def turn(k, c, nb, q):
                at = t_at(k, c, nb)
                bank = t_bank(k, c, nb)
                if isinstance(nb, int) and nb == 0 and (k, c) not in T_TAIL:
                    at -= 1
                if due(at):
                    pe.wait_ge(t_free, at)
                for j in range(TPB):
                    t = TPB * c + j
                    dst = bank[:, P * j:P * j + P]
                    if k == "xT":
                        if j == 0 and c % 2 == 0 and is_it(nb, 0):
                            pe.wait_ge(half_l, c // 2 + 1)
                        elif j == 0 and c == 0:
                            pe.wait_ge(ln_l[0], nb)
                        ins = nc.tensor.transpose(dst, Xs[q][:, t, :].bitcast(F32), ident)
                    if k == "proj":
                        if j == 0:
                            pe.wait_ge(t_free, t_at("xT", c, nb) + 1)
                        ins = nc.tensor.matmul(dst, XT[:, P * j:P * j + P], wqk[:, :], start=True, stop=True)
                    if k == "kT":
                        if j == 0:
                            pe.wait_ge(split, 4 * nb + c + 1)
                        ins = nc.tensor.transpose(dst, QKs[:, j, 2 * D:4 * D].bitcast(F32), ident)
                    if k == "qT":
                        ins = nc.tensor.transpose(dst, QKs[:, j, 0:2 * D].bitcast(F32), ident)
                if k == "mT":
                    pe.wait_ge(nm_ready, 4 * nb + c + 1)
                    ins = nc.tensor.transpose(bank[0:TPB, 0:P], nm[c % 2][:, :], ident)
                ins.then_inc(t_full, 1)

            def piece(n, nb, q, b, s):
                attends = on(b)[0]
                t, g = PIECES[n]
                c = t // TPB
                if t % TPB == 0 and g == 0:
                    pe.wait_ge(dup[c % 2], 64 * (2 * nb + c // 2 + 1))
                bank = max_bank(n, nb, s)
                if isinstance(nb, int) and nb == 0:
                    if n >= sum(MAX_FIRST.values()):
                        pe.wait_ge(m_free, n)
                    elif n >= 5:
                        pe.wait_ge(m_free, n - 4)
                elif n in in_m:
                    at = in_m.index(n)
                    pe.wait_ge(m_free, NM * nb + in_m[at - 1] + 1 - (0 if at else NM))
                if n not in in_m and attends:
                    pe.wait_ge(p_ready, NS * b + s)
                w = min(QB, P * (t + 1) - QB * g)
                last = g == c
                nc_w = max(w, 2 * P)
                ins = nc.tensor.matmul(bank[:, 0:nc_w], Q1[q][:, P * t:P * t + P],
                                       K1[q][:, QB * g:QB * g + nc_w], start=True, stop=not last)
                if last:
                    ins = nc.tensor.matmul(bank[:, w - P:w], identb, edge_q, start=False, stop=True)
                ins.then_inc(m_full, 1)

            def mlp(k, c, b):
                if due(f_at(k, c, b)) and not (is_last(b) and k != "attn"):
                    pe.wait_ge(f_free, f_at(k, c, b))
                bank, x2t, h, w = mlp_buffers(c, b)
                if k == "attn":
                    pe.wait_ge(y_free, 4 * b + c + 1 if c < NF0 else 4 * b + c - 3)
                    for j in range(TPB):
                        ins = nc.tensor.matmul(F[:, P * j:P * j + WOW], YS[:, P * j:P * j + P], wv[:, :],
                                               start=True, stop=True)
                if k == "x2T":
                    if is_last(b):
                        pe.wait_ge(half_l, c // 2 + 3)
                    elif c == 0:
                        pe.wait_ge(ln_l[1], b)
                    for j in range(TPB):
                        ins = nc.tensor.transpose(bank[:, P * j:P * j + P], X2s[:, TPB * c + j, :].bitcast(F32), ident)
                if k == "in":
                    pe.wait_ge(f_free, f_at("x2T", c, b) + 1)
                    nc.tensor.matmul(bank, wi_h[:, :], x2t, start=True, stop=False)
                    ins = nc.tensor.matmul(bank, wi_l[:, :], x2t, start=False, stop=True)
                if k in ("mlp0", "mlp1"):
                    layer = int(k[3])
                    pe.wait_ge(f_free, f_at("in" if layer == 0 else "mlp0", c, b) + 1)
                    if layer == 0:
                        pe.wait_ge(w_in[c % 2], 64 * BATCH if is_last(b) else 32 * (2 * (b - 1) + c // 2 + 1))
                    for r in range(2):
                        cols = slice(ROUTED * r, ROUTED * r + ROUTED)
                        ins = nc.tensor.matmul(bank[:, cols], w[:, r, HID * layer:HID * layer + HID],
                                               h[:, cols], start=True, stop=True)
                if k == "out":
                    pe.wait_ge(f_free, f_at("mlp1", c, b) + 1)
                    for j in range(TPB):
                        ins = nc.tensor.matmul(bank[:, P * j:P * j + WOW], h[:, P * j:P * j + P],
                                               wo_sb[:, :], start=True, stop=True)
                ins.then_inc(f_full, 1)

            def step(b, par, s):
                attends, before, prepares, _ = on(b)
                if s == NS - 1 and is_it(b, 0):
                    pe.wait_ge(ready, 4)
                if s == 0 and is_it(b, 0):
                    pe.wait_ge(m_free, sum(MAX_FIRST.values()))
                if attends:
                    scores(b, par, s)
                todo = [(n, nb, par if left else 1 - par) for n, nb, left in pieces(b, s)]
                half = (len(todo) + 1) // 2
                for point in range(2):
                    if point == 1:
                        lb, lpar, ls = lagging(b, par, s, LAG)
                        if exists(lb):
                            values(lb, lpar, ls)
                    now = todo[half:] if point else todo[:half]
                    if now:
                        piece(*now.pop(0), b, s)
                    for (ev, pt, k, c) in t_events(b):
                        if pt == point and ev == s and prepares:
                            turn(k, c, b + 1, 1 - par)
                        if pt == point and ev - NS == s and attends:
                            turn(k, c, b, par)
                    for one in now:
                        piece(*one, b, s)
                    for (ev, pt, k, c) in f_events(b):
                        if pt == point and ev == s and (attends if k == "attn" and c < NF0 else before):
                            mlp(k, c, b)
            run(pe, prologue, step)

        @block.vector
        def _(dve):
            def prologue():
                v = nc.vector
                dve.wait_ge(ids_in, 16)
                v.tensor_copy(ids_f[:, 0, :], ids_i[:, :])
                v.memset(rows_all[:, P:P + TILES].bitcast(F32), 0.0)
                v.drain()
                v.tensor_scalar(ids_f[:, 1, :], ids_f[:, 0, :], 0.0, float(VOCAB), ALU.is_lt, ALU.mult)
                v.drain()
                v.tensor_tensor(ids_f[:, 0, :], ids_f[:, 0, :], ids_f[:, 1, :], ALU.add)
                v.drain()
                v.tensor_scalar(ids_f[:, 0, :], ids_f[:, 0, :], 0.0, float(VOCAB - 1), ALU.max, ALU.min)
                v.drain()
                v.tensor_scalar(rows_all[:, 0:P], ids_f[:, 0, :], float(HIDDEN // D), float(SLICE), ALU.mult, ALU.add)
                v.drain()
                v.tensor_copy(rows_now[:, :], rows_all[:, 0:TILES]).then_inc(rows_ready, 1)
                v.memset(wo_sb[:, :], 0.0).then_inc(ready, 1)
                v.memset(wv[:, :], 0.0)
                dve.wait_ge(load, 16 * 5)
                v.tensor_scalar(smc[:, 0:D], sm[:, P:P + D], sm[:, P + D - 1:P + D], None, ALU.subtract)
                v.drain()
                v.tensor_copy(smc[:, D:P], smc[:, 0:D]).then_inc(ready, 1)
                v.tensor_copy(conb[:, 0:P], ident)
                v.tensor_copy(conb[:, P:4 * P], con)
                v.tensor_copy(wi_h[:, :], wi_sb[:, :])
                v.drain()
                v.tensor_tensor(wi_l[:, :], wi_sb[:, :], wi_h[:, :].bitcast(F32), ALU.subtract)
                dve.wait_ge(folded, 1)
                v.tensor_scalar(wqk[:, 0:D], T[:, P:P + D], D ** -0.5, None, ALU.mult)
                v.tensor_copy(wqk[:, D:P], T[:, P + D:2 * P])
                v.tensor_copy(wv[:, 0:D], T[:, 2 * P:2 * P + D])
                v.tensor_copy(wv[:, D:D + 1], ident[:, D - 1:D]).then_inc(ready, 1)
                for n in range(2):
                    v.memset(O[n][:, :, :], 0.0).then_inc(out_dma[n], 16)

            def mlp_weights(part):
                v = nc.vector
                if part == 0:
                    dve.wait_ge(load2, 16 * 8)
                    for layer in range(N_LAYERS):
                        w = experts[:, N_EXPERTS, HID * layer:HID * layer + HID]
                        v.tensor_tensor(w, w, ident, ALU.add)
                    v.drain()
                elif part <= N_EXPERTS // 2:
                    e = slice(2 * part - 2, 2 * part)
                    v.tensor_tensor(experts[:, e, :], experts[:, e, :],
                                    experts[:, N_EXPERTS:N_EXPERTS + 1, :].broadcast_to([P, 2, EW]), ALU.add)
                elif part == N_EXPERTS // 2 + 1:
                    v.tensor_copy(route_f[:, 0], route_i[:, :])
                    v.drain()
                    v.tensor_scalar(route_f[:, 1], route_f[:, 0], 0.0, None, ALU.is_ge)
                    v.tensor_scalar(route_f[:, 2], route_f[:, 0], float(N_EXPERTS - 1), None, ALU.is_le)
                    v.drain()
                    v.tensor_tensor(route_f[:, 1], route_f[:, 1], route_f[:, 2], ALU.mult)
                    v.tensor_scalar(route_f[:, 0], route_f[:, 0], -1.0, float(N_EXPERTS), ALU.max, ALU.min)
                    v.drain()
                    v.tensor_scalar(route_f[:, 0], route_f[:, 0], float(-N_EXPERTS), None, ALU.add)
                    v.drain()
                    v.tensor_tensor(route_f[:, 0], route_f[:, 0], route_f[:, 1], ALU.mult)
                    v.drain()
                    v.tensor_scalar(route_e[:, :], route_f[:, 0], float(N_EXPERTS), None, ALU.add).then_inc(ready, 1)

            def sums(n, which, src):
                nc.vector.tensor_reduce(stat[n][:, 2 * which, :], src, AX.X, ALU.add).then_inc(
                    (ln_sum if which == 0 else ln_var)[n], 1)

            def low_part(n, xs):
                nc.vector.tensor_tensor(xs[:, :, D:P], xn[n][:, :, :], xs[:, :, 0:D].bitcast(F32),
                                        ALU.subtract).then_inc(ln_l[n], 1)

            def half_norm(n, h, part):
                v, st, tiles = nc.vector, stat[n], HALF[h]
                src, xs, x, squares = (H1[1] if n else G[0]), (X2s if n else Xs[0]), xn[n], xn[1 - n]
                at = 2 * n + h + 1
                wide = [P, TILES // 2, D]
                if part == 0:
                    if n == 0:
                        dve.wait_ge(gathered if h else gathered0, 16 * TILES // 2)
                    else:
                        v.drain()
                    v.tensor_reduce(st[:, 0, tiles], src[:, tiles, :], AX.X, ALU.add)
                    v.drain()
                    v.tensor_scalar(st[:, 1, tiles], st[:, 0, tiles], 1.0 / D, None, ALU.mult)
                    v.drain()
                    v.tensor_tensor(x[:, tiles, :], src[:, tiles, :],
                                    st[:, 1, tiles].unsqueeze(2).broadcast_to(wide), ALU.subtract).then_inc(half_xc, 1)
                if part == 1:
                    dve.wait_ge(half_sq, at)
                    v.tensor_reduce(st[:, 2, tiles], squares[:, tiles, :], AX.X, ALU.add).then_inc(half_var, 1)
                if part == 2:
                    dve.wait_ge(half_rstd, at)
                    v.tensor_tensor(x[:, tiles, :], x[:, tiles, :],
                                    st[:, 5, tiles].unsqueeze(2).broadcast_to(wide), ALU.mult).then_inc(half_x, 1)
                if part == 3:
                    dve.wait_ge(half_h, at)
                    v.tensor_tensor(xs[:, tiles, D:P], x[:, tiles, :], xs[:, tiles, 0:D].bitcast(F32),
                                    ALU.subtract).then_inc(half_l, 1)

            def reduce_piece(n, nb, s):
                t, g = PIECES[n]
                c = t // TPB
                w = min(QB, P * (t + 1) - QB * g)
                dve.wait_ge(m_full, NM * nb + n + 1)
                nc.vector.tensor_reduce(pm[c % 2][:, t % TPB, g:g + 1], max_bank(n, nb, s)[:, 0:w], AX.X, ALU.max).then_inc(m_free, 1)
                if t % TPB == TPB - 1 and g == c:
                    nc.vector.drain()
                    nc.vector.tensor_reduce(nm[c % 2][:, :], pm[c % 2][:, :, 0:c + 1], AX.X, ALU.max).then_inc(nm_ready, 1)
                    nc.vector.drain()

            def step(b, par, s):
                v = nc.vector
                attends, before, prepares, looks = on(b)
                if is_it(b, 0) and 4 <= s <= 13:
                    mlp_weights(s - 4)
                if s == 0 and looks and not (isinstance(b, int) and b == -2):
                    if is_it(b, -1):
                        dve.wait_ge(gathered0, 16 * TILES // 2)
                    if due(256 * (b + 2) - 128):
                        dve.wait_ge(gathered, 256 * (b + 2) - 128)
                    v.tensor_copy(rows_now[:, :], rows_all[:, bass.ds(TILES * (b + 2), TILES)]).then_inc(rows_ready, 1)
                if s == 17 and looks and not is_it(b, -2):
                    dve.wait_ge(gathered, 256 * (b + 3) - 128)
                    sums(0, 0, G[par][:, :, :])
                if s == 19 and looks and not is_it(b, -2):
                    dve.wait_ge(ln_sq[0], b + 2)
                    sums(0, 1, xn[1][:, :, :])
                todo = pieces(b, s)
                half = (len(todo) + 1) // 2
                for point in range(2):
                    for n, nb, _ in (todo[half:] if point else todo[:half]):
                        reduce_piece(n, nb, s)
                    lb, _, ls = lagging(b, par, s, 1)
                    if point == 0 and s == 9 and before and not is_last(b):
                        dve.wait_ge(ln_h[1], b)
                        low_part(1, X2s)
                    if point == 0 and s == 3 and prepares and not is_it(b, -1):
                        dve.wait_ge(ln_h[0], b + 1)
                        low_part(0, Xs[1 - par])
                    if point == 0 and exists(lb):
                        _, w = cut(ls)
                        dve.wait_ge(p_ready, NS * lb + ls + 1)
                        v.tensor_tensor(prob_l[ls % PBUF][:, 0:w], prob[ls % 2][:, 0:w],
                                        prob_h[ls % PBUF][:, 0:w].bitcast(F32),
                                        ALU.subtract).then_inc(pl_dve, 1)
                    for (ev, pt, k, c) in t_events(b):
                        if point == 0 or not prepares:
                            continue
                        if k == "proj" and ev + 1 == s:
                            dve.wait_ge(roped, 4 * (b + 1) + c + 1)
                            if c > 0:
                                dve.wait_ge(t_full, t_at("qT", c - 1, b + 1) + 1)
                            v.tensor_copy(QKs[:, :, D:3 * D], QK[:, :, :])
                            v.drain()
                            low = QKs[:, :, :].rearrange("p t (f d) -> p t f d", f=4)[:, :, 0:4:3, :]
                            high = QKs[:, :, D:3 * D].rearrange("p t (a d) -> p t a d", a=2)
                            v.tensor_tensor(low, QK[:, :, :].rearrange("p t (a d) -> p t a d", a=2),
                                            high.bitcast(F32), ALU.subtract).then_inc(split, 1)
                        if k == "qT" and c == 3 and ev == s:
                            dve.wait_ge(t_full, t_at("xT", 3, b + 1) + 1)
                            v.memset(Xs[1 - par][:, :, D - 1:D].bitcast(F32), 1.0)
                            v.memset(Xs[1 - par][:, :, P - 1:P].bitcast(F32), 0.0).then_inc(ones_in, 1)
                    for (ev, pt, k, c) in f_events(b):
                        if pt != point or ev != s:
                            continue
                        if k == "attn" and (attends if c < NF0 else before):
                            hb, q = (b, par) if c < NF0 else (b - 1, 1 - par)
                            tiles = slice(TPB * c, TPB * c + TPB)
                            dve.wait_ge(f_full, f_at(k, c, b) + 1)
                            dve.wait_ge(hres_in, 16 * (hb + 1))
                            f = F[:, :].rearrange("p (t n) -> p t n", n=P)
                            v.reciprocal(rec[:, :].unsqueeze(2), f[:, :, D:D + 1])
                            v.drain()
                            v.tensor_tensor(att[:, :, :], f[:, :, 0:D], rec[:, :].unsqueeze(2).broadcast_to([P, TPB, D]),
                                            ALU.mult).then_inc(f_free, 1)
                            v.drain()
                            v.tensor_tensor(H1[q][:, tiles, :], att[:, :, :], H1[q][:, tiles, :],
                                            ALU.add).then_inc(h1_done, 1)
                        if k == "out" and before:
                            dve.wait_ge(f_full, f_at(k, c, b) + 1)
                            dve.wait_ge(h1b_ready, b)
                            dve.wait_ge(out_dma[c % 2], 16 * (2 * (b - 1) + c // 2 + 1))
                            f = mlp_buffers(c, b)[0].rearrange("p (t n) -> p t n", n=P)
                            v.tensor_tensor(O[c % 2][:, :, :], f[:, :, 0:D], H1b[:, TPB * c:TPB * c + TPB, :],
                                            ALU.add).then_inc(o_free if is_last(b) else f_free, 1)

                if is_it(b, 7) and s in (13, 15, 17, 19):
                    half_norm(1, 0, (13, 15, 17, 19).index(s))
                if is_last(b) and s == 2:
                    for part in range(4):
                        half_norm(1, 1, part)
                if is_it(b, -2) and s == 5:
                    for part in range(4):
                        half_norm(0, 0, part)
                if is_it(b, -1) and s in (1, 6, 7, 8):
                    half_norm(0, 1, (1, 6, 7, 8).index(s))
                if s == 2 and before and not is_last(b):
                    v.drain()
                    sums(1, 0, H1[1 - par][:, :, :])
                if s == 5 and before and not is_last(b):
                    dve.wait_ge(ln_sq[1], b)
                    sums(1, 1, xn[0][:, :, :])
            run(dve, prologue, step)


_DTYPES = {"float32": F32, "int32": I32}


def shape_constants():
    k, q = np.arange(P)[:, None], np.arange(P)[None, :]
    edge = np.where(k > q, np.float32(NEG), np.float32(0))
    full = np.full((P, P), NEG, np.float32)
    consts = np.concatenate([np.eye(P, dtype=np.float32), full, edge, edge.T], axis=1)
    half = ROPE // 2
    theta = np.float32(1.0) / np.float32(10000.0) ** (np.arange(half, dtype=np.float32) / np.float32(half))
    angle = (np.arange(SEQ, dtype=np.float32)[:, None] * theta[None, :]).astype(np.float32)
    sin, cos = np.sin(angle), np.cos(angle)
    cos2 = np.repeat(cos, 2, axis=1)
    sin2 = np.stack([-sin, sin], axis=-1).reshape(SEQ, ROPE)
    tabs = np.stack([cos2, sin2]).reshape(2, TILES, P, 1, ROPE)
    tabs = np.broadcast_to(tabs, (2, TILES, P, 2, ROPE)).transpose(2, 0, 1, 3, 4)
    return np.ascontiguousarray(consts, np.float32), np.ascontiguousarray(tabs, np.float32)


def kernel(**inputs):
    import concourse.bacc as _bacc
    from concourse.bass_utils import run_bass_kernel_spmd as _run

    a = {k: np.asarray(v) for k, v in inputs.items()}
    at, ff = "L0_attn_", "L0_ffn_"
    consts, rope = shape_constants()
    wq, wkv = a[at + "Wq_comp"].T, a[at + "Wkv_comp"].T
    small = np.concatenate([wq, wq, wkv, wkv, a[at + "Wqc"], a[at + "Wqr"], a[at + "Wkc"], a[at + "Wkr"],
                            a[at + "Wv"]], axis=1)
    wit = a[ff + "Wi"].T
    arrays = {
        "ids": a["x"].reshape(P, P).T,
        "table": a["L0_tok_ple_table"],
        "consts": consts,
        "rope": rope,
        "small": small,
        "wi": np.concatenate([wit, wit], axis=0),
        "wo": a[ff + "Wo"].T,
        "wr": a[ff + "Wr"].transpose(3, 1, 0, 2).reshape(P, N_EXPERTS, N_LAYERS * HID),
        "ws": a[ff + "Ws"][:, 0].transpose(2, 0, 1).reshape(P, N_LAYERS * HID),
        "brt": a[ff + "br"].transpose(2, 1, 0),
        "bst": a[ff + "bs"][:, 0].T,
        "bi": a[ff + "bi"].reshape(P, 1),
        "bo": np.broadcast_to(a[ff + "bo"], (P, D)),
        "route": a[ff + "route_id"].reshape(1, 64),
    }
    nc = _bacc.Bacc("TRN2", target_bir_lowering=False, num_devices=1)
    feeds, args = {}, []
    for name, v in arrays.items():
        v = np.ascontiguousarray(v)
        feeds[f"in_{name}"] = v
        args.append(nc.dram_tensor(f"in_{name}", v.shape, _DTYPES[v.dtype.name], kind="ExternalInput").ap())
    args.append(nc.dram_tensor("out_0", (BATCH, SEQ, D), F32, kind="ExternalOutput").ap())
    tower_kernel(nc, *args)
    r = _run(nc, [feeds], core_ids=[0])
    return r.results[0]["out_0"]
```
